# Optimizing a Trainium2 kernel written in Bass

```python
import numpy as np
import jax
import jax.numpy as jnp

def _softmax(x, axis=-1):
    return jax.nn.softmax(x, axis=axis)

def _gelu(x):
    return jax.nn.gelu(x, approximate=True)

def _silu(x):
    return jax.nn.silu(x)

def _sigmoid(x):
    return jax.nn.sigmoid(x)

def _layernorm(x, axis=-1, eps=1e-05):
    m = jnp.mean(x, axis=axis, keepdims=True)
    v = jnp.var(x, axis=axis, keepdims=True)
    return (x - m) / jnp.sqrt(v + eps)

def _scatter_add(tgt, idx, src, axis=0):
    return tgt.at[idx].add(src)

def _segment_sum(src, seg, n):
    return jax.ops.segment_sum(src, seg, n)
kernel_name = 'mk_gnn_preln_d2_gnn_r64_4edf25'

def setup_inputs(seed: int=0):
    np.random.seed(seed)
    _w = jnp.asarray

    def _rec_inputs():
        import jax
        import jax.numpy as jnp
        _gk = jax.random.key(seed)
        x = -0.000202 + 1 * jax.random.normal(jax.random.fold_in(_gk, 1), (100000, 64), jnp.float32)
        src = jax.random.randint(jax.random.fold_in(_gk, 2), (25000,), 0, 100000, jnp.int32)
        dst = jnp.minimum((100000 * jax.random.uniform(jax.random.fold_in(_gk, 3), (25000,)) ** 2.0).astype(jnp.int32), 99999)
        _o = jnp.argsort(dst, stable=True)
        src = src[_o]
        dst = dst[_o]
        edge_attr_32 = -5.3897e-05 + 0.999841 * jax.random.normal(jax.random.fold_in(_gk, 12), (25000, 32), jnp.float32)
        return (x, src, dst, edge_attr_32)
    x, src, dst, edge_attr_32 = _rec_inputs()

    def _L0_gnn_setup():
        import jax, jax.numpy as jnp
        import numpy as np
        N_NODES = 100000
        N_EDGES = 25000
        IN_FEAT = 64
        OUT_FEAT = 64
        key = jax.random.key(seed)
        k1, k2, k3, k4, k5 = jax.random.split(key, 5)
        h = jax.random.normal(k1, (N_NODES, IN_FEAT), dtype=jnp.float32)
        src = jax.random.randint(k2, (N_EDGES,), 0, N_NODES, dtype=jnp.int32)
        dst = jax.random.randint(k3, (N_EDGES,), 0, N_NODES, dtype=jnp.int32)
        W = jax.random.normal(k4, (OUT_FEAT, 2 * IN_FEAT), dtype=jnp.float32) * (1.0 / np.sqrt(2 * IN_FEAT))
        b = jax.random.normal(k5, (OUT_FEAT,), dtype=jnp.float32) * 0.01
        return {'h': h, 'src': src, 'dst': dst, 'W': W, 'b': b}
    _L0_gnn_all = _L0_gnn_setup()
    _L0_gnn_in = {k: v for k, v in _L0_gnn_all.items() if k in ('W', 'b')}
    del _L0_gnn_all

    def _L1_gnn_setup():
        import jax, jax.numpy as jnp
        import numpy as np
        N_NODES, N_EDGES = (50000, 12500)
        NODE_DIM, EDGE_DIM, HIDDEN, NUM_LAYERS = (64, 32, 64, 2)
        IN_MSG = NODE_DIM + EDGE_DIM
        IN_UPD = NODE_DIM + HIDDEN
        key = jax.random.key(seed)
        ks = jax.random.split(key, 12)

        def w(k, shape, fan_in):
            return jax.random.normal(k, shape, jnp.float32) * (1.0 / np.sqrt(fan_in))
        return {'node_features': jax.random.normal(ks[0], (N_NODES, NODE_DIM), jnp.float32), 'edge_features': jax.random.normal(ks[1], (N_EDGES, EDGE_DIM), jnp.float32), 'msg_w1': w(ks[2], (NUM_LAYERS, IN_MSG, HIDDEN), IN_MSG), 'msg_b1': w(ks[3], (NUM_LAYERS, HIDDEN), IN_MSG), 'msg_w2': w(ks[4], (NUM_LAYERS, HIDDEN, HIDDEN), HIDDEN), 'msg_b2': w(ks[5], (NUM_LAYERS, HIDDEN), HIDDEN), 'upd_w1': w(ks[6], (IN_UPD, HIDDEN), IN_UPD), 'upd_b1': w(ks[7], (HIDDEN,), IN_UPD), 'upd_w2': w(ks[8], (HIDDEN, NODE_DIM), HIDDEN), 'upd_b2': w(ks[9], (NODE_DIM,), HIDDEN), 'src': jax.random.randint(ks[10], (N_EDGES,), 0, N_NODES, dtype=jnp.int32), 'dst': jax.random.randint(ks[11], (N_EDGES,), 0, N_NODES, dtype=jnp.int32)}
    _L1_gnn_all = _L1_gnn_setup()
    _L1_gnn_in = {k: v for k, v in _L1_gnn_all.items() if k in ('msg_w1', 'msg_b1', 'msg_w2', 'msg_b2', 'upd_w1', 'upd_b1', 'upd_w2', 'upd_b2')}
    del _L1_gnn_all
    return {'x': x, 'src': src, 'dst': dst, 'edge_attr_32': edge_attr_32, 'L0_gnn_W': _L0_gnn_in['W'], 'L0_gnn_b': _L0_gnn_in['b'], 'L1_gnn_msg_w1': _L1_gnn_in['msg_w1'], 'L1_gnn_msg_b1': _L1_gnn_in['msg_b1'], 'L1_gnn_msg_w2': _L1_gnn_in['msg_w2'], 'L1_gnn_msg_b2': _L1_gnn_in['msg_b2'], 'L1_gnn_upd_w1': _L1_gnn_in['upd_w1'], 'L1_gnn_upd_b1': _L1_gnn_in['upd_b1'], 'L1_gnn_upd_w2': _L1_gnn_in['upd_w2'], 'L1_gnn_upd_b2': _L1_gnn_in['upd_b2']}

def reference(x, src, dst, edge_attr_32, L0_gnn_W, L0_gnn_b, L1_gnn_msg_w1, L1_gnn_msg_b1, L1_gnn_msg_w2, L1_gnn_msg_b2, L1_gnn_upd_w1, L1_gnn_upd_b1, L1_gnn_upd_w2, L1_gnn_upd_b2):
    import jax
    import jax.numpy as jnp

    def _L0_gnn_ref(h, src, dst, W, b):
        import jax, jax.numpy as jnp
        import numpy as np
        N_NODES = 100000
        N_EDGES = 25000
        IN_FEAT = 64
        OUT_FEAT = 64
        N = h.shape[0]
        msgs = h[src]
        sums = jax.ops.segment_sum(msgs, dst, num_segments=N)
        deg = jax.ops.segment_sum(jnp.ones((src.shape[0],), h.dtype), dst, num_segments=N)
        h_N = sums / jnp.maximum(deg, 1.0)[:, None]
        h_total = jnp.concatenate([h, h_N], axis=1)
        return h_total @ W.T + b

    def _L1_gnn_ref(node_features, edge_features, msg_w1, msg_b1, msg_w2, msg_b2, upd_w1, upd_b1, upd_w2, upd_b2, src, dst):
        import jax, jax.numpy as jnp
        import numpy as np
        N_NODES, N_EDGES = (50000, 12500)
        NODE_DIM, EDGE_DIM, HIDDEN, NUM_LAYERS = (64, 32, 64, 2)
        IN_MSG = NODE_DIM + EDGE_DIM
        IN_UPD = NODE_DIM + HIDDEN
        n_nodes = node_features.shape[0]
        combined = jnp.concatenate([node_features[src], edge_features], axis=-1)
        msg = jnp.zeros((combined.shape[0], msg_w2.shape[-1]), combined.dtype)
        for l in range(msg_w1.shape[0]):
            h = jax.nn.relu(combined @ msg_w1[l] + msg_b1[l])
            msg = msg + (h @ msg_w2[l] + msg_b2[l])
        agg = jax.ops.segment_sum(msg, dst, num_segments=n_nodes)
        deg = jax.ops.segment_sum(jnp.ones((dst.shape[0],), msg.dtype), dst, num_segments=n_nodes)
        agg = agg / (deg[:, None] + 1e-08)
        comb2 = jnp.concatenate([node_features, agg], axis=-1)
        return jax.nn.relu(comb2 @ upd_w1 + upd_b1) @ upd_w2 + upd_b2
    h = jnp.maximum(_layernorm(x, axis=-1), 0.0)
    x = x + _L0_gnn_ref(h, src, dst, L0_gnn_W, L0_gnn_b)
    h = jnp.maximum(_layernorm(x, axis=-1), 0.0)
    x = x + _L1_gnn_ref(h, edge_attr_32, L1_gnn_msg_w1, L1_gnn_msg_b1, L1_gnn_msg_w2, L1_gnn_msg_b2, L1_gnn_upd_w1, L1_gnn_upd_b1, L1_gnn_upd_w2, L1_gnn_upd_b2, src, dst)
    return x

_drawn_inputs = setup_inputs


def setup_inputs(seed=0):
    import zlib

    import numpy as np

    out = dict(_drawn_inputs(seed))
    spreads = {}
    factors = {'L0_gnn_b': 6.54}
    for name, (base, spread) in spreads.items():
        noise = np.random.default_rng([zlib.crc32(name.encode()), seed]).standard_normal(out[name].shape)
        drawn = base * np.exp(spread * noise) if base else spread * noise
        out[name] = jnp.asarray(drawn.astype(out[name].dtype))
    for name, factor in factors.items():
        out[name] = (out[name] * factor).astype(out[name].dtype)
    return out
```

```python
import concourse.bass as bass
from concourse import mybir
from collections import namedtuple
from contextlib import ExitStack

FP32 = mybir.dt.float32
I32 = mybir.dt.int32
ALU = mybir.AluOpType
ACT = mybir.ActivationFunctionType
AX = mybir.AxisListType


def gnn_program(nc, x, src, dst, edge_attr, gnn_w, gnn_b, msg_w1, msg_b1, msg_w2, msg_b2,
                upd_w1, upd_b1, upd_w2, upd_b2, out):
    N, D = x.shape
    E = src.shape[0]
    DE = edge_attr.shape[1]
    P = 128
    G = 16
    CHUNK = P * G
    NFULL = N // CHUNK
    STEPS = NFULL + 1
    PREST = (N - NFULL * CHUNK) // G
    assert PREST * G + NFULL * CHUNK == N
    Q = 4
    T = STEPS * Q
    assert (T - Q) * P < E <= T * P
    EPAD = T * P
    TF = E // P
    EREST = E - TF * P
    H = T // 2
    UNROLL = 4
    assert STEPS % UNROLL == 1
    GD = G * D
    QD = Q * D
    NBLK = GD // P
    R1 = D + 1
    EPS = 1e-5
    SENT = 1 << 17

    x1_d = nc.dram_tensor("x1_scratch", (N + EPAD, D), FP32, kind="Internal").ap()
    agg_d = nc.dram_tensor("agg_scratch", (N + EPAD, D), FP32, kind="Internal").ap()

    ctx = ExitStack()
    with ctx:
        def sb(name, shape, dt=FP32):
            return ctx.enter_context(nc.sbuf_tensor(name, shape, dt))

        def pb(name, cols):
            return ctx.enter_context(nc.psum_tensor(name, [P, cols], FP32))

        def sem(name):
            return ctx.enter_context(nc.semaphore(name))

        def sems(name, n):
            return [sem(f"{name}{k}") for k in range(n)]

        ident = sb("ident", [P, P])
        zeros = sb("zeros", [P, GD])
        ones = sb("ones", [1, P])
        sel = sb("sel", [P, 2])
        rows_i = [sb(f"rows_i{k}", [H, 2 * P], I32) for k in range(3)]
        rows_f = [sb(f"rows_f{k}", [H, 2 * P]) for k in range(3)]
        src_idx = sb("src_idx", [P, T], I32)
        end_idx = sb("end_idx", [P, T], I32)
        dst_f = sb("dst_f", [P, T])
        next_f = sb("next_f", [P, T])
        spare_f = sb("spare_f", [P, T])
        spare_i = sb("spare_i", [P, T], I32)
        dst_pair = sb("dst_pair", [P, T, 2])
        w_raw = sb("w_raw", [P, 2, P])
        w_bd = sb("w_bd", [P, 2, P])
        u1_bd = sb("u1_bd", [P, P])
        u2_bd = sb("u2_bd", [P, P])
        w1h = sb("w1h", [P, 2, P])
        w1e = sb("w1e", [P, Q, P])
        w2 = sb("w2", [P, D])
        w2t = sb("w2t", [D, P])
        u1b = sb("u1b", [D, D])
        w2u = sb("w2u", [P, D])
        b2c = sb("b2c", [D, 2])
        b2sum = sb("b2sum", [D, P])
        b2u = sb("b2u", [1, Q, D])
        b1c = sb("b1c", [P, 1])
        ub1c = sb("ub1c", [P, 1])
        brow = sb("brow", [1, 2, D])
        gb = sb("gb", [1, NBLK, D])
        ub2 = sb("ub2", [1, NBLK, D])

        edge_rows = sb("edge_rows", [P, T * D])
        xin = [sb(f"xin{k}", [P, GD]) for k in range(UNROLL)]
        agg = [sb(f"agg{k}", [P, GD]) for k in range(2)]
        xc = sb("xc", [P, GD])
        sq = sb("sq", [P, GD])
        h = [sb(f"h{k}", [P, GD]) for k in range(2)]
        hT = [sb(f"hT{k}", [P, GD]) for k in range(2)]
        xce = sb("xce", [P, QD])
        sqe = sb("sqe", [P, QD])
        he = [sb(f"he{k}", [P, QD]) for k in range(2)]
        hTe = [sb(f"hTe{k}", [P, QD]) for k in range(2)]
        stats = sb("stats", [P, 3, G + Q])
        stat = stats[:, :, 0:G]
        state = stats[:, :, G:G + Q]
        eps = sb("eps", [P, 1])
        cols = [sb(f"cols{k}", [P, Q, 2]) for k in range(2)]
        same = [sb(f"same{k}", [P, Q, 2, P]) for k in range(2)]
        msg = [sb(f"msg{k}", [P, Q, R1]) for k in range(2)]
        run = [sb(f"run{k}", [P, Q, R1]) for k in range(2)]
        rdeg = sb("rdeg", [P, 2 * Q])
        ea = [sb(f"ea{k}", [P, Q * DE]) for k in range(UNROLL)]
        eaT = [sb(f"eaT{k}", [P, P]) for k in range(2)]
        hid = [sb(f"hid{k}", [P, Q * P]) for k in range(2)]

        psD = pb("psD", 512)
        psT = [pb(f"psT{k}", 512) for k in range(2)]
        psY = pb("psY", 1024)
        psE = pb("psE", 512)
        psR = pb("psR", 512)
        psH = pb("psH", 512)

        def wait(eng, s, value):
            if not isinstance(value, int) or value > 0:
                eng.wait_ge(s, value)

        def steps(eng, body, peel=1):
            turns = STEPS // UNROLL
            for u in range(UNROLL):
                body(u, 0, u)
            with eng.Fori(1, turns + 1 - peel) as k:
                for u in range(UNROLL):
                    body(k * UNROLL + u, k, u)
            for k in range(turns + 1 - peel, turns):
                for u in range(UNROLL):
                    body(k * UNROLL + u, k, u)
            body(STEPS - 1, turns, 0)

        FILLED_ROWS = 3
        psP = [psD, psH]

        w_loaded = sem("w_loaded")
        rows_loaded = sem("rows_loaded")
        filled = sem("filled")
        pool_const = sem("pool_const")
        rows_conv = sem("rows_conv")
        idxT = sem("idxT")
        prep = sem("prep")
        w_prep = sem("w_prep")
        w_pe = sem("w_pe")
        run_filled = sem("run_filled")
        idx_ready = sem("idx_ready")
        spare_zeroed = sem("spare_zeroed")
        agg_zeroed = sem("agg_zeroed")

        a_x = sems("a_x", UNROLL)
        a_gath = sems("a_gath", UNROLL)
        a_stored = sems("a_stored", UNROLL)
        a_scat = sems("a_scat", UNROLL)
        b_x = sems("b_x", UNROLL)
        b_agg = sems("b_agg", 2)
        b_gath = sems("b_gath", UNROLL)
        b_ea = sems("b_ea", UNROLL)
        b_scat = sems("b_scat", UNROLL)
        b_stored = sems("b_stored", UNROLL)

        def stage(prefix, names):
            return namedtuple(prefix, names)(*(sem(f"{prefix}_{n}") for n in names))

        LN = ["sum", "xc", "sq", "ss", "std", "rstd", "h"]
        SEG = ["cols", "dstb", "same", "msg", "run_pe", "run", "deg", "rdeg", "rows"]
        ad = stage("ad", LN + ["tr0", "tr1", "hT0", "hT1", "y0", "y1", "x1"])
        ae = stage("ae", LN + SEG + ["tr", "hT", "w"])
        bd = stage("bd", LN + ["tr0", "tr1", "hT0", "hT1", "p0", "p1", "r0", "r1", "y0", "y1", "out"])
        be = stage("be", LN + SEG + ["tr", "hT", "eatr", "eaT", "hid_pe", "hid", "w"])

        fills = [(zeros, 0.0), (w_raw, 0.0), (u1_bd, 0.0), (u2_bd, 0.0), (w1h, 0.0), (w1e, 0.0), (ones, 1.0), (eps, EPS)]
        FILLED_ALL = FILLED_ROWS + len(fills)
        RUN_FILLED = 3
        W_DMAS = 2 * (2 + 2 + 2 + 2) + 2 * Q + 5
        SPARE_DMAS = -(-(EPAD // P) // G)

        block = ctx.enter_context(nc.Block())

        def node_chunk(t, i):
            return t[bass.ds(i * CHUNK, CHUNK), :].rearrange("(p g) d -> p (g d)", p=P)

        def node_rest(t):
            return t[NFULL * CHUNK:N, :].rearrange("(p g) d -> p (g d)", p=PREST)

        @block.sync
        def _(sp):
            sp.wait_ge(filled, FILLED_ROWS)
            for k, (v, first) in enumerate(((src, 0), (dst, 0), (dst, 1))):
                n = E - first
                full = n // P
                rest = n - full * P
                sp.dma_start(rows_i[k][:, 0:P], v[first:first + H * P].rearrange("(q c) -> q c", c=P)
                             ).then_inc(rows_loaded, 16)
                sp.dma_start(rows_i[k][0:full - H, P:2 * P],
                             v[first + H * P:first + full * P].rearrange("(q c) -> q c", c=P)
                             ).then_inc(rows_loaded, 16)
                sp.dma_start(rows_i[k][full - H:full - H + 1, P:P + rest],
                             v[first + full * P:first + n].rearrange("(q c) -> q c", q=1)
                             ).then_inc(rows_loaded, 16)

            sp.wait_ge(filled, FILLED_ALL)
            for a in range(2):
                lo = a * D
                for half in range(2):
                    sp.dma_start(w_raw[lo:lo + D, half, lo:lo + D], gnn_w[:, half * D:(half + 1) * D]
                                 ).then_inc(w_loaded, 16)
                sp.dma_start(u1_bd[lo:lo + D, lo:lo + D], upd_w1[0:D, :]).then_inc(w_loaded, 16)
                sp.dma_start(u2_bd[lo:lo + D, lo:lo + D], upd_w2[:, :]).then_inc(w_loaded, 16)
                for layer in range(2):
                    sp.dma_start(w1h[lo:lo + D, a, layer * D:(layer + 1) * D], msg_w1[layer, 0:D, :]
                                 ).then_inc(w_loaded, 16)
                sp.dma_start(ub1c[lo:lo + D, :], upd_b1.rearrange("(f o) -> f o", o=1)).then_inc(w_loaded, 16)
                sp.dma_start(b2c[:, a:a + 1], msg_b2[a, :].rearrange("(f o) -> f o", o=1)
                             ).then_inc(w_loaded, 16)
            for q in range(Q):
                for layer in range(2):
                    sp.dma_start(w1e[q * DE:(q + 1) * DE, q, layer * D:(layer + 1) * D],
                                 msg_w1[layer, D:D + DE, :]).then_inc(w_loaded, 16)
            sp.dma_start(w2[:, :], msg_w2.rearrange("l f o -> (l f) o")).then_inc(w_loaded, 16)
            sp.dma_start(u1b[:, :], upd_w1[D:2 * D, :]).then_inc(w_loaded, 16)
            sp.dma_start(b1c[:, :], msg_b1.rearrange("l (f o) -> (l f) o", o=1)).then_inc(w_loaded, 16)
            sp.dma_start(brow[:, 0, :], gnn_b.rearrange("(o f) -> o f", o=1)).then_inc(w_loaded, 16)
            sp.dma_start(brow[:, 1, :], upd_b2.rearrange("(o f) -> o f", o=1)).then_inc(w_loaded, 16)

            def load_x(t, i, k, u, landed):
                if isinstance(i, int) and i == STEPS - 1:
                    sp.dma_start(xin[u][0:PREST, :], node_rest(t)).then_inc(landed[u], 16)
                else:
                    sp.dma_start(xin[u][:, :], node_chunk(t, i)).then_inc(landed[u], 16)

            def store_x(t, i, u, stored):
                if isinstance(i, int) and i == STEPS - 1:
                    sp.dma_start(node_rest(t), xin[u][0:PREST, :]).then_inc(stored[u], 16)
                else:
                    sp.dma_start(node_chunk(t, i), xin[u][:, :]).then_inc(stored[u], 16)

            load_x(x, 0, 0, 0, a_x)
            load_x(x, 1, 0, 1, a_x)
            per = EPAD // P
            spare = x1_d[N:N + EPAD, :].rearrange("(p g) d -> p g d", p=P)
            for g0 in range(0, per, G):
                g1 = min(per, g0 + G)
                sp.dma_start(spare[:, g0:g1, :], zeros[:, 0:(g1 - g0) * D].rearrange("p (g d) -> p g d", d=D)
                             ).then_inc(spare_zeroed, 16)

            def step_a(i, k, u):
                v = (u + 2) % UNROLL
                kv = k + (u + 2) // UNROLL
                wait(sp, a_stored[v], kv * 16)
                if not (isinstance(i, int) and i + 2 >= STEPS):
                    load_x(x, i + 2 if not isinstance(i, int) or i + 2 < NFULL else STEPS - 1, kv, v, a_x)
                if isinstance(i, int) and i == STEPS - 1:
                    sp.dma_start(node_rest(agg_d), zeros[0:PREST, :]).then_inc(agg_zeroed, 16)
                else:
                    sp.dma_start(node_chunk(agg_d, i), zeros[:, :]).then_inc(agg_zeroed, 16)
                sp.wait_ge(ad.x1, i + 1)
                store_x(x1_d, i, u, a_stored)

            steps(sp, step_a, peel=2)

            for u in range(UNROLL):
                sp.wait_ge(a_stored[u], 16 * ((STEPS - 1 - u) // UNROLL + 1))
                sp.wait_ge(a_scat[u], 16 * Q * ((STEPS - 1 - u) // UNROLL + 1))
            def step_ea(i, k, u):
                wait(sp, be.eatr, i - UNROLL + 1)
                if isinstance(i, int) and i == STEPS - 1:
                    e0 = i * Q * P
                    nf = TF - i * Q
                    sp.dma_start(ea[u][:, 0:nf * DE].rearrange("p (q c) -> p q c", c=DE),
                                 edge_attr[e0:e0 + nf * P, :].rearrange("(q p) c -> p q c", p=P)
                                 ).then_inc(b_ea[u], 16)
                    sp.dma_start(ea[u][0:EREST, nf * DE:(nf + 1) * DE], edge_attr[e0 + nf * P:E, :]
                                 ).then_inc(b_ea[u], 16)
                else:
                    sp.dma_start(ea[u][:, :].rearrange("p (q c) -> p q c", c=DE),
                                 edge_attr[bass.ds(i * (Q * P), Q * P), :].rearrange("(q p) c -> p q c", p=P)
                                 ).then_inc(b_ea[u], 16)

            steps(sp, step_ea)

            sp.wait_ge(agg_zeroed, 16 * STEPS)
            for u in range(UNROLL):
                sp.wait_ge(b_scat[u], 16 * Q * ((STEPS - 1 - u) // UNROLL + 1))

            def load_agg(i, s):
                if isinstance(i, int) and i == STEPS - 1:
                    sp.dma_start(agg[s][0:PREST, :], node_rest(agg_d)).then_inc(b_agg[s], 16)
                else:
                    sp.dma_start(agg[s][:, :], node_chunk(agg_d, i)).then_inc(b_agg[s], 16)

            load_x(x1_d, 0, 0, 0, b_x)
            load_agg(0, 0)
            load_x(x1_d, 1, 0, 1, b_x)

            def step_b(i, k, u):
                v = (u + 2) % UNROLL
                kv = k + (u + 2) // UNROLL
                wait(sp, b_stored[v], kv * 16)
                if not (isinstance(i, int) and i + 2 >= STEPS):
                    load_x(x1_d, i + 2 if not isinstance(i, int) or i + 2 < NFULL else STEPS - 1, kv, v, b_x)
                if not (isinstance(i, int) and i + 1 >= STEPS):
                    wait(sp, bd.p1, i)
                    load_agg(i + 1 if not isinstance(i, int) or i + 1 < NFULL else STEPS - 1, (u + 1) % 2)
                sp.wait_ge(bd.out, i + 1)
                store_x(out, i, u, b_stored)

            steps(sp, step_b, peel=2)
            for u in range(UNROLL):
                sp.wait_ge(b_stored[u], 16 * ((STEPS - 1 - u) // UNROLL + 1))

        def norm_sum(s, xv, st):
            nc.vector.tensor_reduce(st[:, 0, :], xv, AX.X, ALU.add).then_inc(s.sum, 1)

        def norm_center(dve, s, i, xv, st, centered, free=None):
            n = xv.shape[1]
            wait(dve, free or s.h, i)
            dve.wait_ge(s.sum, i + 1)
            nc.vector.scalar_tensor_tensor(out=centered[:, :].rearrange("p (g d) -> p g d", d=D),
                                           in0=st[:, 0, :].unsqueeze(2).to_broadcast([P, n, D]), scalar=-1.0 / D,
                                           in1=xv, op0=ALU.mult, op1=ALU.add).then_inc(s.xc, 1)

        def norm_square(act, s, i, centered, squared):
            act.wait_ge(s.xc, i + 1)
            wait(act, s.ss, i)
            nc.scalar.activation(squared[:, :], centered[:, :], ACT.Square, scale=D ** -0.5).then_inc(s.sq, 1)

        def norm_var(dve, s, i, squared, st):
            dve.wait_ge(s.sq, i + 1)
            nc.vector.tensor_reduce(st[:, 1, :], squared[:, :].rearrange("p (g d) -> p g d", d=D), AX.X,
                                    ALU.add).then_inc(s.ss, 1)

        def norm_std(act, s, i, st):
            act.wait_ge(s.ss, i + 1)
            nc.scalar.activation(st[:, 1, :], st[:, 1, :], ACT.Sqrt, bias=eps[:, 0:1]).then_inc(s.std, 1)

        def norm_rstd(dve, s, i, st):
            dve.wait_ge(s.std, i + 1)
            nc.vector.reciprocal(st[:, 2, :], st[:, 1, :]).then_inc(s.rstd, 1)

        def norm_relu(dve, s, i, centered, st, to, done=None):
            n = st.shape[2]
            dve.wait_ge(s.rstd, i + 1)
            nc.vector.scalar_tensor_tensor(out=to[:, :].rearrange("p (g d) -> p g d", d=D),
                                           in0=centered[:, :].rearrange("p (g d) -> p g d", d=D), scalar=0.0,
                                           in1=st[:, 2, :].unsqueeze(2).to_broadcast([P, n, D]),
                                           op0=ALU.max, op1=ALU.mult).then_inc(done or s.h, 1)

        def transposes(to, of, n, done):
            for j in range(n):
                last = nc.tensor.transpose(to[:, j * P:(j + 1) * P], of[:, j * P:(j + 1) * P], ident[:, :])
            last.then_inc(done, 1)

        def dst_columns(i, b):
            return nc.vector.tensor_copy(cols[b][:, :, :], dst_pair[:, bass.ds(i * Q, Q), :])

        def dst_rows(pe, s, i, b):
            pe.wait_ge(s.cols, i + 1)
            wait(pe, s.same, i)
            for q in range(Q):
                last = nc.tensor.transpose(psD[:, q * P:(q + 1) * P], cols[b][:, q, 0:1].to_broadcast([P, P]),
                                           ident[:, :])
            last.then_inc(s.dstb, 1)

        def dst_compare(dve, s, i, b):
            dve.wait_ge(s.dstb, i + 1)
            wait(dve, s.run_pe, Q * (i - 1))
            nc.vector.tensor_tensor(
                same[b][:, :, :, :],
                psD[:, :].rearrange("p (q o e) -> p q o e", q=Q, o=1).to_broadcast([P, Q, 2, P]),
                cols[b][:, :, :].unsqueeze(3).to_broadcast([P, Q, 2, P]), ALU.is_equal).then_inc(s.same, 1)

        def dst_sums(pe, s, i, b):
            pe.wait_ge(s.same, i + 1)
            pe.wait_ge(s.msg, i + 1)
            for q in range(Q):
                to = psR[:, q * R1:(q + 1) * R1]
                before = run[b][:, q - 1, :] if q else run[1 - b][:, Q - 1, :]
                wait(pe, s.run, i * Q + q)
                nc.tensor.matmul(to, same[b][:, q, 0, :], msg[b][:, q, :], start=True, stop=False)
                nc.tensor.matmul(to, same[b][:, q, 1, :], before, start=False, stop=True).then_inc(s.run_pe, 1)

        def dst_sums_out(act, s, i, b):
            wait(act, s.rows, i - 1)
            for q in range(Q):
                act.wait_ge(s.run_pe, i * Q + q + 1)
                nc.scalar.copy(run[b][:, q, :], psR[:, q * R1:(q + 1) * R1]).then_inc(s.run, 1)

        def dst_rows_out(dve, s, i, b, op, by):
            dve.wait_ge(s.run, (i + 1) * Q)
            nc.vector.tensor_scalar(rdeg[:, 0:Q], run[b][:, :, D], by, None, op).then_inc(s.deg, 1)
            dve.wait_ge(s.deg, i + 1)
            nc.vector.reciprocal(rdeg[:, Q:2 * Q], rdeg[:, 0:Q]).then_inc(s.rdeg, 1)
            dve.wait_ge(s.rdeg, i + 1)
            nc.vector.tensor_tensor(edge_rows[:, bass.ds(i * QD, QD)].rearrange("p (q d) -> p q d", d=D),
                                    run[b][:, :, 0:D], rdeg[:, Q:2 * Q].unsqueeze(2).to_broadcast([P, Q, D]),
                                    ALU.mult).then_inc(s.rows, 1)

        @block.gpsimd
        def _(pool):
            nc.gpsimd.memset(ident[:, :], 1.0).then_inc(pool_const, 1)
            nc.gpsimd.memset(sel[:, :], 1.0).then_inc(pool_const, 1)
            nc.gpsimd.iota(spare_i[:, :], [[P, T]], base=N, channel_multiplier=1).then_inc(pool_const, 1)
            pool.wait_ge(pool_const, 3)
            nc.gpsimd.affine_select(out=ident[:, :], in_=ident[:, :], pattern=[[-1, P]], compare_op=ALU.is_equal,
                                    fill=0.0, base=0, channel_multiplier=1).then_inc(pool_const, 1)
            nc.gpsimd.affine_select(out=sel[:, 0:1], in_=sel[:, 0:1], pattern=[[0, 1]], compare_op=ALU.is_equal,
                                    fill=0.0, base=1 - P, channel_multiplier=1).then_inc(pool_const, 1)

            def gather(table, j, landed):
                wait(pool, landed[j % UNROLL], 16 * Q * (j // UNROLL))
                for t in range(j * Q, (j + 1) * Q):
                    nc.gpsimd.indirect_dma_start(
                        out=edge_rows[:, t * D:(t + 1) * D], out_offset=None, in_=table,
                        in_offset=bass.IndirectOffsetOnAxis(ap=src_idx[:, t:t + 1], axis=0)
                    ).then_inc(landed[j % UNROLL], 16)

            def scatter(table, j, landed, op):
                wait(pool, landed[j % UNROLL], 16 * Q * (j // UNROLL))
                for t in range(j * Q, (j + 1) * Q):
                    nc.gpsimd.indirect_dma_start(
                        out=table, out_offset=bass.IndirectOffsetOnAxis(ap=end_idx[:, t:t + 1], axis=0),
                        in_=edge_rows[:, t * D:(t + 1) * D], in_offset=None, compute_op=op
                    ).then_inc(landed[j % UNROLL], 16)

            pool.wait_ge(idx_ready, 2)
            for j in range(STEPS):
                gather(x[:, :], j, a_gath)
            pool.wait_ge(spare_zeroed, 16 * SPARE_DMAS)
            for u in range(UNROLL):
                pool.wait_ge(a_stored[u], 16 * ((STEPS - 1 - u) // UNROLL + 1))
            for j in range(STEPS):
                pool.wait_ge(ae.rows, j + 1)
                scatter(x1_d[:, :], j, a_scat, ALU.add)
            for u in range(UNROLL):
                pool.wait_ge(a_scat[u], 16 * Q * ((STEPS - 1 - u) // UNROLL + 1))
            for j in range(STEPS):
                gather(x1_d[:, :], j, b_gath)
            pool.wait_ge(agg_zeroed, 16 * STEPS)
            for j in range(STEPS):
                pool.wait_ge(be.rows, j + 1)
                scatter(agg_d[:, :], j, b_scat, ALU.bypass)

        @block.vector
        def _(dve):
            for k, pad in enumerate((0, SENT, SENT)):
                nc.vector.memset(rows_i[k][:, :], pad).then_inc(filled, 1)
            for t, v in fills:
                nc.vector.memset(t[:], v).then_inc(filled, 1)
            nc.vector.memset(run[1][:, :, :], 0.0).then_inc(run_filled, 1)
            for k in range(2):
                nc.vector.memset(msg[k][:, :, D:R1], 1.0).then_inc(run_filled, 1)

            dve.wait_ge(rows_loaded, 16 * 9)
            for k in range(3):
                nc.vector.tensor_copy(rows_f[k][:, :], rows_i[k][:, :]).then_inc(rows_conv, 1)
            dve.wait_ge(pool_const, 5)
            nc.vector.tensor_copy(spare_f[:, :], spare_i[:, :]).then_inc(prep, 1)
            nc.vector.tensor_scalar(sel[:, 1:2], sel[:, 0:1], 1.0, None, ALU.subtract).then_inc(prep, 1)
            dve.wait_ge(idxT, 1)
            nc.vector.tensor_copy(src_idx[:, :], psH[:, 0:T]).then_inc(idx_ready, 1)
            dve.wait_ge(idxT, 2)
            nc.vector.tensor_copy(dst_f[:, :], psE[:, 0:T]).then_inc(prep, 1)
            nc.vector.tensor_copy(dst_pair[:, :, 0], psE[:, 0:T]).then_inc(prep, 1)
            dve.wait_ge(idxT, 3)
            nc.vector.tensor_copy(next_f[:, :], psR[:, 0:T]).then_inc(prep, 1)
            nc.vector.memset(dst_pair[:, 0:1, 1], -1.0).then_inc(prep, 1)
            dve.wait_ge(prep, 6)
            nc.vector.tensor_scalar(dst_pair[:, 1:T, 1], dst_f[:, 0:T - 1], sel[:, 0:1], sel[:, 1:2],
                                    ALU.mult, ALU.add).then_inc(prep, 1)
            dve.wait_ge(prep, 7)
            nc.vector.tensor_tensor(next_f[:, :], next_f[:, :], dst_f[:, :], ALU.not_equal).then_inc(prep, 1)
            nc.vector.tensor_tensor(dst_f[:, :], dst_f[:, :], spare_f[:, :], ALU.subtract).then_inc(prep, 1)
            dve.wait_ge(prep, 9)
            nc.vector.tensor_tensor(dst_f[:, :], dst_f[:, :], next_f[:, :], ALU.mult).then_inc(prep, 1)
            dve.wait_ge(prep, 10)
            nc.vector.tensor_tensor(end_idx[:, :], dst_f[:, :], spare_f[:, :], ALU.add).then_inc(idx_ready, 1)

            dve.wait_ge(w_loaded, 16 * W_DMAS)
            nc.vector.tensor_tensor(b2sum[:, :], b2c[:, 0:1].to_broadcast([D, P]), b2c[:, 1:2].to_broadcast([D, P]),
                                    ALU.add).then_inc(w_prep, 1)
            nc.vector.tensor_copy(gb[:, :, :], brow[:, 0:1, :].to_broadcast([1, NBLK, D])).then_inc(w_prep, 1)
            nc.vector.tensor_copy(ub2[:, :, :], brow[:, 1:2, :].to_broadcast([1, NBLK, D])).then_inc(w_prep, 1)
            dve.wait_ge(w_pe, 1)
            nc.vector.tensor_copy(w_bd[:, :, :], psT[0][:, 0:2 * P].rearrange("p (a c) -> p a c", a=2)
                                  ).then_inc(w_prep, 1)
            nc.vector.tensor_copy(w2t[:, :], psT[1][0:D, 0:P]).then_inc(w_prep, 1)
            dve.wait_ge(w_pe, 2)
            nc.vector.tensor_copy(w2u[:, :], psY[:, 0:D]).then_inc(w_prep, 1)
            nc.vector.tensor_copy(b2u[:, :, :], psY[0:1, D:2 * D].unsqueeze(1).to_broadcast([1, Q, D])
                                  ).then_inc(w_prep, 1)

            def edge_view(i):
                return edge_rows[:, bass.ds(i * QD, QD)].rearrange("p (q d) -> p q d", d=D)

            def node_view(u):
                return xin[u][:, :].rearrange("p (g d) -> p g d", d=D)

            def finish_a(i, u):
                dve.wait_ge(ad.y1, i + 1)
                nc.vector.tensor_tensor(xin[u][:, :], psY[:, :], xin[u][:, :], ALU.add).then_inc(ad.x1, 1)
                dst_rows_out(dve, ae, i, u % 2, ALU.max, 1.0)

            def step_a(i, k, u):
                b = u % 2
                dst_columns(i, b).then_inc(ae.cols, 1)
                dve.wait_ge(a_x[u], 16 * (k + 1))
                norm_sum(ad, node_view(u), stat)
                dve.wait_ge(a_gath[u], 16 * Q * (k + 1))
                norm_sum(ae, edge_view(i), state)
                norm_center(dve, ad, i, node_view(u), stat, xc)
                norm_center(dve, ae, i, edge_view(i), state, xce)
                norm_var(dve, ad, i, sq, stat)
                norm_var(dve, ae, i, sqe, state)
                dst_compare(dve, ae, i, b)
                norm_rstd(dve, ae, i, stats)
                wait(dve, ad.tr1, i - 1)
                norm_relu(dve, ae, i, xc, stat, h[b], ad.h)
                wait(dve, ae.tr, i - 1)
                norm_relu(dve, ae, i, xce, state, he[b])
                if not isinstance(i, int) or i:
                    finish_a(i - 1, (u - 1) % UNROLL)

            steps(dve, step_a)
            finish_a(STEPS - 1, 0)

            def step_be(i, k, u):
                b = u % 2
                dst_columns(i, b).then_inc(be.cols, 1)
                dve.wait_ge(b_gath[u], 16 * Q * (k + 1))
                norm_sum(be, edge_view(i), state)
                norm_center(dve, be, i, edge_view(i), state, xce)
                dst_compare(dve, be, i, b)
                norm_var(dve, be, i, sqe, state)
                norm_rstd(dve, be, i, state)
                wait(dve, be.tr, i - 1)
                norm_relu(dve, be, i, xce, state, he[b])
                if not isinstance(i, int) or i:
                    dst_rows_out(dve, be, i - 1, 1 - b, ALU.add, 1e-8)

            steps(dve, step_be)
            dst_rows_out(dve, be, STEPS - 1, 0, ALU.add, 1e-8)

            def finish_b(i, u):
                dve.wait_ge(bd.y1, i + 1)
                nc.vector.tensor_tensor(xin[u][:, :], psY[:, :], xin[u][:, :], ALU.add).then_inc(bd.out, 1)

            def step_bd(i, k, u):
                dve.wait_ge(b_x[u], 16 * (k + 1))
                norm_sum(bd, node_view(u), stat)
                norm_center(dve, bd, i, node_view(u), stat, xc)
                if not isinstance(i, int) or i:
                    finish_b(i - 1, (u - 1) % UNROLL)
                norm_var(dve, bd, i, sq, stat)
                norm_rstd(dve, bd, i, stat)
                wait(dve, bd.tr1, i - 1)
                norm_relu(dve, bd, i, xc, stat, h[u % 2])

            steps(dve, step_bd)
            finish_b(STEPS - 1, 0)

        @block.scalar
        def _(act):
            def transposed_out(s, i, b):
                for half in range(2):
                    act.wait_ge((s.tr0, s.tr1)[half], i + 1)
                    nc.scalar.copy(hT[b][:, half * 512:(half + 1) * 512], psT[half][:, :]
                                   ).then_inc((s.hT0, s.hT1)[half], 1)

            def step_a(i, k, u):
                b = u % 2
                norm_square(act, ad, i, xc, sq)
                norm_square(act, ae, i, xce, sqe)
                act.wait_ge(ad.ss, i + 1)
                norm_std(act, ae, i, stats)
                wait(act, ad.y1, i - 1)
                transposed_out(ad, i, b)
                act.wait_ge(ae.tr, i + 1)
                wait(act, ae.w, i - 1)
                nc.scalar.copy(hTe[b][:, :], psE[:, 0:QD]).then_inc(ae.hT, 1)
                act.wait_ge(ae.w, i + 1)
                wait(act, ae.run_pe, Q * (i - 1))
                if isinstance(i, int) and i < 2:
                    act.wait_ge(run_filled, RUN_FILLED)
                nc.scalar.copy(msg[b][:, :, 0:D], psH[:, 0:QD].rearrange("p (q d) -> p q d", d=D)
                               ).then_inc(ae.msg, 1)
                dst_sums_out(act, ae, i, b)

            steps(act, step_a)

            def step_be(i, k, u):
                b = u % 2
                norm_square(act, be, i, xce, sqe)
                norm_std(act, be, i, state)
                act.wait_ge(be.eatr, i + 1)
                wait(act, be.hid_pe, i - 1)
                nc.scalar.copy(hTe[b][:, :], psE[:, 0:QD]).then_inc(be.hT, 1)
                nc.scalar.copy(eaT[b][:, :], psE[:, QD:QD + P]).then_inc(be.eaT, 1)
                act.wait_ge(be.hid_pe, i + 1)
                wait(act, be.w, i - 1)
                nc.scalar.activation(hid[b][:, :], psH[:, :], ACT.Relu, bias=b1c[:, 0:1]).then_inc(be.hid, 1)
                act.wait_ge(be.w, i + 1)
                wait(act, be.run_pe, Q * (i - 1))
                nc.scalar.copy(msg[b][:, :, 0:D], psY[:, 0:QD].rearrange("p (q d) -> p q d", d=D)
                               ).then_inc(be.msg, 1)
                dst_sums_out(act, be, i, b)

            steps(act, step_be)

            def step_bd(i, k, u):
                norm_square(act, bd, i, xc, sq)
                norm_std(act, bd, i, stat)
                wait(act, bd.p1, i - 1)
                transposed_out(bd, i, u % 2)
                for half in range(2):
                    act.wait_ge((bd.p0, bd.p1)[half], i + 1)
                    wait(act, (bd.y0, bd.y1)[half], i)
                    nc.scalar.activation(hid[half][:, :], psP[half][:, :], ACT.Relu, bias=ub1c[:, 0:1]
                                         ).then_inc((bd.r0, bd.r1)[half], 1)

            steps(act, step_bd)

        @block.tensor
        def _(pe):
            pe.wait_ge(pool_const, 4)
            for k, to in enumerate((psH, psE, psR)):
                pe.wait_ge(rows_conv, k + 1)
                for a in range(2):
                    last = nc.tensor.transpose(to[:, a * H:(a + 1) * H], rows_f[k][:, a * P:(a + 1) * P],
                                               ident[0:H, 0:H])
                last.then_inc(idxT, 1)
            pe.wait_ge(w_loaded, 16 * W_DMAS)
            for half in range(2):
                nc.tensor.transpose(psT[0][:, half * P:(half + 1) * P], w_raw[:, half, :], ident[:, :])
            nc.tensor.transpose(psT[1][0:D, 0:P], w2[:, :], ident[:, :]).then_inc(w_pe, 1)
            pe.wait_ge(w_prep, 5)
            nc.tensor.matmul(psY[:, 0:D], w2t[:, :], u1b[:, :], start=True, stop=True)
            nc.tensor.matmul(psY[:, D:2 * D], b2sum[:, :], u1b[:, :], start=True, stop=True).then_inc(w_pe, 1)
            pe.wait_ge(w_prep, 7)
            pe.wait_ge(idx_ready, 2)

            def norm_transposes(s, i, b):
                pe.wait_ge(s.h, i + 1)
                for half in range(2):
                    wait(pe, (s.hT0, s.hT1)[half], i)
                    transposes(psT[half], h[b][:, half * 512:(half + 1) * 512], 4, (s.tr0, s.tr1)[half])

            def by_nodes(s, i, sources, weights, bias, ready, done, read):
                for half in range(2):
                    wait(pe, read, i)
                    nc.tensor.matmul(psY[:, half * 512:(half + 1) * 512], ones[0:1, :],
                                     bias[0:1, :, :], start=True, stop=False)
                    pe.wait_ge(ready[half], i + 1)
                    for j in range(4):
                        last = nc.tensor.matmul(psY[:, half * 512 + j * P:half * 512 + (j + 1) * P],
                                                sources[half][:, j * P:(j + 1) * P], weights,
                                                start=False, stop=j == 3)
                    last.then_inc(done[half], 1)

            def step_a(i, k, u):
                b = u % 2
                dst_rows(pe, ae, i, b)
                norm_transposes(ad, i, b)
                pe.wait_ge(ae.h, i + 1)
                wait(pe, ae.hT, i)
                transposes(psE[:, 0:QD], he[b], 2, ae.tr)
                by_nodes(ad, i, (hT[b][:, 0:512], hT[b][:, 512:1024]), w_bd[:, 0, :], gb, (ad.hT0, ad.hT1),
                         (ad.y0, ad.y1), ad.x1)
                pe.wait_ge(ae.hT, i + 1)
                wait(pe, ae.msg, i)
                for j in range(2):
                    last = nc.tensor.matmul(psH[:, j * P:(j + 1) * P], hTe[b][:, j * P:(j + 1) * P],
                                            w_bd[:, 1, :], start=True, stop=True)
                last.then_inc(ae.w, 1)
                dst_sums(pe, ae, i, b)

            steps(pe, step_a)

            def step_be(i, k, u):
                b = u % 2
                dst_rows(pe, be, i, b)
                pe.wait_ge(be.h, i + 1)
                wait(pe, be.eaT, i)
                transposes(psE[:, 0:QD], he[b], 2, be.tr)
                pe.wait_ge(b_ea[u], 16 * (k + 1) if not (isinstance(i, int) and i == STEPS - 1) else 16 * (k + 2))
                transposes(psE[:, QD:QD + P], ea[u], 1, be.eatr)
                pe.wait_ge(be.hT, i + 1)
                wait(pe, be.hid, i)
                for a in range(2):
                    nc.tensor.matmul(psH[:, a * QD:(a + 1) * QD], w1h[:, a, :], hTe[b][:, :], start=a == 0,
                                     stop=False)
                pe.wait_ge(be.eaT, i + 1)
                for q in range(Q):
                    at = ((q % 2) * 2 + q // 2) * P
                    last = nc.tensor.matmul(psH[:, at:at + P], w1e[:, q, :], eaT[b][:, :], start=False,
                                            stop=q == Q - 1)
                last.then_inc(be.hid_pe, 1)
                wait(pe, be.msg, i)
                nc.tensor.matmul(psY[:, 0:QD], ones[0:1, :], b2u[0:1, :, :], start=True, stop=False)
                pe.wait_ge(be.hid, i + 1)
                for q in range(Q):
                    at = ((q % 2) * 2 + q // 2) * P
                    last = nc.tensor.matmul(psY[:, q * D:(q + 1) * D], hid[b][:, at:at + P], w2u[:, :],
                                            start=False, stop=q == Q - 1)
                last.then_inc(be.w, 1)
                dst_sums(pe, be, i, b)

            steps(pe, step_be)

            def step_bd(i, k, u):
                b = u % 2
                norm_transposes(bd, i, b)
                pe.wait_ge(b_agg[b], 16 * (k * 2 + u // 2 + 1))
                for half in range(2):
                    pe.wait_ge((bd.hT0, bd.hT1)[half], i + 1)
                    wait(pe, (bd.r0, bd.r1)[half], i)
                    nc.tensor.matmul(psP[half][:, :], u1_bd[:, :], hT[b][:, half * 512:(half + 1) * 512],
                                     start=True, stop=False)
                    for j in range(4):
                        at = half * 512 + j * P
                        last = nc.tensor.matmul(psP[half][:, j * P:(j + 1) * P], agg[b][:, at:at + P],
                                                ident[:, :], start=False, stop=j == 3)
                    last.then_inc((bd.p0, bd.p1)[half], 1)
                by_nodes(bd, i, hid, u2_bd[:, :], ub2, (bd.r0, bd.r1), (bd.y0, bd.y1), bd.out)

            steps(pe, step_bd)


_INS = ['x', 'src', 'dst', 'edge_attr_32', 'L0_gnn_W', 'L0_gnn_b', 'L1_gnn_msg_w1', 'L1_gnn_msg_b1',
        'L1_gnn_msg_w2', 'L1_gnn_msg_b2', 'L1_gnn_upd_w1', 'L1_gnn_upd_b1', 'L1_gnn_upd_w2', 'L1_gnn_upd_b2']


def kernel(**inputs):
    import numpy as _np
    import concourse.bacc as _bacc
    from concourse import mybir as _mybir
    from concourse.bass_utils import run_bass_kernel_spmd as _run

    nc = _bacc.Bacc("TRN2", target_bir_lowering=False, num_devices=1)
    arrays, args = {}, []
    for name in _INS:
        a = _np.ascontiguousarray(inputs[name])
        arrays[f"in_{name}"] = a
        args.append(nc.dram_tensor(f"in_{name}", a.shape, _mybir.dt.from_np(a.dtype), kind="ExternalInput").ap())
    shape = inputs['x'].shape
    args.append(nc.dram_tensor("out", shape, _mybir.dt.float32, kind="ExternalOutput").ap())
    gnn_program(nc, *args)
    r = _run(nc, [arrays], core_ids=[0])
    return r.results[0]["out"]
```

```python
import concourse.bass as bass
from concourse import mybir
from collections import namedtuple
from contextlib import ExitStack

FP32 = mybir.dt.float32
I32 = mybir.dt.int32
BF16 = mybir.dt.bfloat16
ALU = mybir.AluOpType
ACT = mybir.ActivationFunctionType
AX = mybir.AxisListType


def gnn_program(nc, x, src, dst, edge_attr, gnn_w, gnn_b, msg_w1, msg_b1, msg_w2, msg_b2,
                upd_w1, upd_b1, upd_w2, upd_b2, out):
    N, D = x.shape
    E = src.shape[0]
    DE = edge_attr.shape[1]
    P = 128
    G = 16
    CHUNK = P * G
    NFULL = N // CHUNK
    STEPS = NFULL + 1
    PREST = (N - NFULL * CHUNK) // G
    assert PREST * G + NFULL * CHUNK == N
    Q = 4
    T = STEPS * Q
    assert (T - Q) * P < E <= T * P
    EPAD = T * P
    TF = E // P
    EREST = E - TF * P
    H = T // 2
    UNROLL = 4
    assert STEPS % UNROLL == 1
    GD = G * D
    QD = Q * D
    NBLK = GD // P
    R1 = D + 1
    EPS = 1e-5
    SENT = 1 << 17

    x1_d = nc.dram_tensor("x1_scratch", (N + EPAD, D), FP32, kind="Internal").ap()
    agg_d = nc.dram_tensor("agg_scratch", (N + EPAD, D), FP32, kind="Internal").ap()

    ctx = ExitStack()
    with ctx:
        def sb(name, shape, dt=FP32):
            return ctx.enter_context(nc.sbuf_tensor(name, shape, dt))

        def pb(name, cols):
            return ctx.enter_context(nc.psum_tensor(name, [P, cols], FP32))

        def sem(name):
            return ctx.enter_context(nc.semaphore(name))

        def sems(name, n):
            return [sem(f"{name}{k}") for k in range(n)]

        ident = sb("ident", [P, P])
        zeros = sb("zeros", [P, GD])
        ones = sb("ones", [1, P])
        ones3 = sb("ones3", [3, P], BF16)
        sel = sb("sel", [P, 2])
        rows_i = [sb(f"rows_i{k}", [H, 2 * P], I32) for k in range(3)]
        rows_f = [sb(f"rows_f{k}", [H, 2 * P]) for k in range(3)]
        src_idx = sb("src_idx", [P, T], I32)
        end_idx = sb("end_idx", [P, T], I32)
        dst_f = sb("dst_f", [P, T])
        next_f = sb("next_f", [P, T])
        spare_f = sb("spare_f", [P, T])
        spare_i = sb("spare_i", [P, T], I32)
        dst_pair = sb("dst_pair", [P, T, 2])
        w_raw = sb("w_raw", [P, 2, P])
        w_bd = sb("w_bd", [P, 2, P])
        u1_bd = sb("u1_bd", [P, P])
        u2_bd = sb("u2_bd", [P, P])
        w1h = sb("w1h", [P, 2, P])
        w1e = sb("w1e", [P, Q, P])
        w2 = sb("w2", [P, D])
        w2t = sb("w2t", [D, P])
        u1b = sb("u1b", [D, D])
        w2u = sb("w2u", [P, D])
        b2c = sb("b2c", [D, 2])
        b2sum = sb("b2sum", [D, P])
        b2u = sb("b2u", [1, Q, D])
        b1c = sb("b1c", [P, 1])
        ub1c = sb("ub1c", [P, 1])
        brow = sb("brow", [1, 2, D])
        left = sb("left", [1, 2, D])
        parts = sb("parts", [1, 2, 3, NBLK, D], BF16)
        bias3 = sb("bias3", [3, 2, NBLK * D], BF16)
        first_f = sb("first_f", [1, STEPS + 1])
        bound_i = sb("bound_i", [1, STEPS], I32)
        bound_f = sb("bound_f", [1, STEPS])
        less = sb("less", [1, STEPS, STEPS])
        need_f = sb("need_f", [1, 2, STEPS])
        need = sb("need", [1, 2, STEPS], I32)

        edge_rows = sb("edge_rows", [P, T * D])
        xin = [sb(f"xin{k}", [P, GD]) for k in range(UNROLL)]
        agg = [sb(f"agg{k}", [P, GD]) for k in range(2)]
        xc = [sb(f"xc{k}", [P, GD]) for k in range(2)]
        sq = sb("sq", [P, GD])
        h = [sb(f"h{k}", [P, GD]) for k in range(2)]
        hT = [sb(f"hT{k}", [P, GD]) for k in range(2)]
        xce = [sb(f"xce{k}", [P, QD]) for k in range(2)]
        sqe = sb("sqe", [P, QD])
        he = [sb(f"he{k}", [P, QD]) for k in range(2)]
        hTe = [sb(f"hTe{k}", [P, QD]) for k in range(2)]
        stats = sb("stats", [P, 3, G + Q])
        stat = stats[:, :, 0:G]
        state = stats[:, :, G:G + Q]
        eps = sb("eps", [P, 1])
        cols = [sb(f"cols{k}", [P, Q, 2]) for k in range(2)]
        same = [sb(f"same{k}", [P, Q, 2, P]) for k in range(2)]
        msg = [sb(f"msg{k}", [P, Q, R1]) for k in range(2)]
        run = [sb(f"run{k}", [P, Q, R1]) for k in range(2)]
        rdeg = sb("rdeg", [P, 2 * Q])
        ea = [sb(f"ea{k}", [P, Q * DE]) for k in range(UNROLL)]
        eaT = [sb(f"eaT{k}", [P, P]) for k in range(2)]
        hid = [sb(f"hid{k}", [P, Q * P]) for k in range(2)]

        psD = pb("psD", 512)
        psT = [pb(f"psT{k}", 512) for k in range(2)]
        psY = pb("psY", 1024)
        psE = pb("psE", 512)
        psR = pb("psR", 512)
        psH = pb("psH", 512)

        def wait(eng, s, value):
            if not isinstance(value, int) or value > 0:
                eng.wait_ge(s, value)

        def real(i):
            return not isinstance(i, int) or 0 <= i < STEPS

        def steps(eng, body, peel=2):
            turns = STEPS // UNROLL
            for u in range(UNROLL):
                body(u, 0, u)
            with eng.Fori(1, turns + 1 - peel) as k:
                for u in range(UNROLL):
                    body(k * UNROLL + u, k, u)
            for k in range(turns + 1 - peel, turns):
                for u in range(UNROLL):
                    body(k * UNROLL + u, k, u)
            body(STEPS - 1, turns, 0)

        FILLED_ROWS = 3
        psP = [psD, psH]

        w_loaded = sem("w_loaded")
        rows_loaded = sem("rows_loaded")
        filled = sem("filled")
        pool_const = sem("pool_const")
        rows_conv = sem("rows_conv")
        idxT = sem("idxT")
        prep = sem("prep")
        w_prep = sem("w_prep")
        w_pe = sem("w_pe")
        bias_loaded = sem("bias_loaded")
        bias_split = sem("bias_split")
        bias_moved = sem("bias_moved")
        need_ready = sem("need_ready")
        x1_landed = sem("x1_landed")
        agg_landed = sem("agg_landed")
        run_filled = sem("run_filled")
        idx_ready = sem("idx_ready")
        spare_zeroed = sem("spare_zeroed")
        agg_zeroed = sem("agg_zeroed")

        a_x = sems("a_x", UNROLL)
        a_gath = sems("a_gath", UNROLL)
        a_stored = sems("a_stored", UNROLL)
        a_scat = sems("a_scat", UNROLL)
        b_x = sems("b_x", UNROLL)
        b_agg = sems("b_agg", 2)
        b_gath = sems("b_gath", UNROLL)
        b_ea = sems("b_ea", UNROLL)
        b_scat = sems("b_scat", UNROLL)
        b_stored = sems("b_stored", UNROLL)

        def stage(prefix, names):
            return namedtuple(prefix, names)(*(sem(f"{prefix}_{n}") for n in names))

        LN = ["sum", "xc", "sq", "ss", "std", "rstd", "h"]
        SEG = ["cols", "dstb", "same", "msg", "run_pe", "run", "deg", "rdeg", "rows"]
        ad = stage("ad", LN + ["tr0", "tr1", "hT0", "hT1", "y0", "y1", "x1_0", "x1"])
        ae = stage("ae", LN + SEG + ["tr", "hT", "w"])
        bd = stage("bd", LN + ["tr0", "tr1", "hT0", "hT1", "p0", "p1", "r0", "r1", "y0", "y1", "out"])
        be = stage("be", LN + SEG + ["tr", "hT", "eatr", "eaT", "hid_pe", "hid", "w"])

        fills = [(zeros, 0.0), (w_raw, 0.0), (u1_bd, 0.0), (u2_bd, 0.0), (w1h, 0.0), (w1e, 0.0), (ones, 1.0), (eps, EPS), (ones3, 1.0)]
        FILLED_ALL = FILLED_ROWS + len(fills)
        RUN_FILLED = 3
        W_DMAS = 2 * (2 + 2 + 2 + 2) + 2 * Q + 3
        SPARE_DMAS = -(-(EPAD // P) // G)

        block = ctx.enter_context(nc.Block())

        def node_chunk(t, i):
            return t[bass.ds(i * CHUNK, CHUNK), :].rearrange("(p g) d -> p (g d)", p=P)

        def node_rest(t):
            return t[NFULL * CHUNK:N, :].rearrange("(p g) d -> p (g d)", p=PREST)

        @block.sync
        def _(sp):
            sp.wait_ge(filled, FILLED_ROWS)
            for k, (v, first) in enumerate(((src, 0), (dst, 0), (dst, 1))):
                n = E - first
                full = n // P
                rest = n - full * P
                sp.dma_start(rows_i[k][:, 0:P], v[first:first + H * P].rearrange("(q c) -> q c", c=P)
                             ).then_inc(rows_loaded, 16)
                sp.dma_start(rows_i[k][0:full - H, P:2 * P],
                             v[first + H * P:first + full * P].rearrange("(q c) -> q c", c=P)
                             ).then_inc(rows_loaded, 16)
                sp.dma_start(rows_i[k][full - H:full - H + 1, P:P + rest],
                             v[first + full * P:first + n].rearrange("(q c) -> q c", q=1)
                             ).then_inc(rows_loaded, 16)

            sp.dma_start(brow[:, 0, :], gnn_b.rearrange("(o f) -> o f", o=1)).then_inc(bias_loaded, 16)
            sp.dma_start(brow[:, 1, :], upd_b2.rearrange("(o f) -> o f", o=1)).then_inc(bias_loaded, 16)
            sp.wait_ge(bias_split, 7)
            for n in range(2):
                for part in range(3):
                    sp.dma_start(bias3[part:part + 1, n, :], parts[0:1, n, part, :, :].rearrange("p a d -> p (a d)")
                                 ).then_inc(bias_moved, 16)
            sp.wait_ge(filled, FILLED_ALL)
            for a in range(2):
                lo = a * D
                for half in range(2):
                    sp.dma_start(w_raw[lo:lo + D, half, lo:lo + D], gnn_w[:, half * D:(half + 1) * D]
                                 ).then_inc(w_loaded, 16)
                sp.dma_start(u1_bd[lo:lo + D, lo:lo + D], upd_w1[0:D, :]).then_inc(w_loaded, 16)
                sp.dma_start(u2_bd[lo:lo + D, lo:lo + D], upd_w2[:, :]).then_inc(w_loaded, 16)
                for layer in range(2):
                    sp.dma_start(w1h[lo:lo + D, a, layer * D:(layer + 1) * D], msg_w1[layer, 0:D, :]
                                 ).then_inc(w_loaded, 16)
                sp.dma_start(ub1c[lo:lo + D, :], upd_b1.rearrange("(f o) -> f o", o=1)).then_inc(w_loaded, 16)
                sp.dma_start(b2c[:, a:a + 1], msg_b2[a, :].rearrange("(f o) -> f o", o=1)
                             ).then_inc(w_loaded, 16)
            for q in range(Q):
                for layer in range(2):
                    sp.dma_start(w1e[q * DE:(q + 1) * DE, q, layer * D:(layer + 1) * D],
                                 msg_w1[layer, D:D + DE, :]).then_inc(w_loaded, 16)
            sp.dma_start(w2[:, :], msg_w2.rearrange("l f o -> (l f) o")).then_inc(w_loaded, 16)
            sp.dma_start(u1b[:, :], upd_w1[D:2 * D, :]).then_inc(w_loaded, 16)
            sp.dma_start(b1c[:, :], msg_b1.rearrange("l (f o) -> (l f) o", o=1)).then_inc(w_loaded, 16)

            def load_x(t, i, k, u, landed):
                if isinstance(i, int) and i == STEPS - 1:
                    sp.dma_start(xin[u][0:PREST, :], node_rest(t)).then_inc(landed[u], 16)
                else:
                    sp.dma_start(xin[u][:, :], node_chunk(t, i)).then_inc(landed[u], 16)

            def store_x(t, i, u, stored):
                if isinstance(i, int) and i == STEPS - 1:
                    sp.dma_start(node_rest(t), xin[u][0:PREST, :]).then_inc(stored[u], 16)
                else:
                    sp.dma_start(node_chunk(t, i), xin[u][:, :]).then_inc(stored[u], 16)

            load_x(x, 0, 0, 0, a_x)
            load_x(x, 1, 0, 1, a_x)
            load_x(x, 2, 0, 2, a_x)
            per = EPAD // P
            spare = x1_d[N:N + EPAD, :].rearrange("(p g) d -> p g d", p=P)
            for g0 in range(0, per, G):
                g1 = min(per, g0 + G)
                sp.dma_start(spare[:, g0:g1, :], zeros[:, 0:(g1 - g0) * D].rearrange("p (g d) -> p g d", d=D)
                             ).then_inc(spare_zeroed, 16)

            def step_a(i, k, u):
                v = (u + 3) % UNROLL
                kv = k + (u + 3) // UNROLL
                if real(i - 1):
                    sp.wait_ge(a_stored[v], kv * 16)
                    sp.sem_inc(x1_landed, 1)
                if real(i + 3):
                    load_x(x, i + 3, kv, v, a_x)
                if isinstance(i, int) and i == STEPS - 1:
                    sp.dma_start(node_rest(agg_d), zeros[0:PREST, :]).then_inc(agg_zeroed, 16)
                else:
                    sp.dma_start(node_chunk(agg_d, i), zeros[:, :]).then_inc(agg_zeroed, 16)
                sp.wait_ge(ad.x1, i + 1)
                store_x(x1_d, i, u, a_stored)

            steps(sp, step_a)

            sp.wait_ge(a_stored[(STEPS - 1) % UNROLL], 16 * ((STEPS - 1) // UNROLL + 1))
            sp.sem_inc(x1_landed, 1)
            for u in range(UNROLL):
                sp.wait_ge(a_scat[u], 16 * Q * ((STEPS - 1 - u) // UNROLL + 1))
            def step_ea(i, k, u):
                wait(sp, be.eatr, i - UNROLL + 1)
                if isinstance(i, int) and i == STEPS - 1:
                    e0 = i * Q * P
                    nf = TF - i * Q
                    sp.dma_start(ea[u][:, 0:nf * DE].rearrange("p (q c) -> p q c", c=DE),
                                 edge_attr[e0:e0 + nf * P, :].rearrange("(q p) c -> p q c", p=P)
                                 ).then_inc(b_ea[u], 16)
                    sp.dma_start(ea[u][0:EREST, nf * DE:(nf + 1) * DE], edge_attr[e0 + nf * P:E, :]
                                 ).then_inc(b_ea[u], 16)
                else:
                    sp.dma_start(ea[u][:, :].rearrange("p (q c) -> p q c", c=DE),
                                 edge_attr[bass.ds(i * (Q * P), Q * P), :].rearrange("(q p) c -> p q c", p=P)
                                 ).then_inc(b_ea[u], 16)

            steps(sp, step_ea)

            def load_agg(i, s):
                sp.wait_ge(agg_landed, sp.value_load(need[0:1, 1, bass.ds(i, 1)], min_val=1, max_val=STEPS))
                if isinstance(i, int) and i == STEPS - 1:
                    sp.dma_start(agg[s][0:PREST, :], node_rest(agg_d)).then_inc(b_agg[s], 16)
                else:
                    sp.dma_start(agg[s][:, :], node_chunk(agg_d, i)).then_inc(b_agg[s], 16)

            load_x(x1_d, 0, 0, 0, b_x)
            load_agg(0, 0)
            load_x(x1_d, 1, 0, 1, b_x)
            load_x(x1_d, 2, 0, 2, b_x)

            def step_b(i, k, u):
                v = (u + 3) % UNROLL
                kv = k + (u + 3) // UNROLL
                wait(sp, b_stored[v], kv * 16)
                if real(i + 3):
                    load_x(x1_d, i + 3, kv, v, b_x)
                if not (isinstance(i, int) and i + 1 >= STEPS):
                    wait(sp, bd.p1, i)
                    load_agg(i + 1 if not isinstance(i, int) or i + 1 < NFULL else STEPS - 1, (u + 1) % 2)
                sp.wait_ge(bd.out, i + 1)
                store_x(out, i, u, b_stored)

            steps(sp, step_b)
            for u in range(UNROLL):
                sp.wait_ge(b_stored[u], 16 * ((STEPS - 1 - u) // UNROLL + 1))

        def norm_sum(dve, s, i, xv, st):
            wait(dve, s.xc, i)
            nc.vector.tensor_reduce(st[:, 0, :], xv, AX.X, ALU.add).then_inc(s.sum, 1)

        def norm_center(dve, s, i, xv, st, centered):
            n = xv.shape[1]
            wait(dve, s.h, i - 1)
            dve.wait_ge(s.sum, i + 1)
            nc.vector.scalar_tensor_tensor(out=centered[:, :].rearrange("p (g d) -> p g d", d=D),
                                           in0=st[:, 0, :].unsqueeze(2).to_broadcast([P, n, D]), scalar=-1.0 / D,
                                           in1=xv, op0=ALU.mult, op1=ALU.add).then_inc(s.xc, 1)

        def norm_square(act, s, i, centered, squared):
            act.wait_ge(s.xc, i + 1)
            wait(act, s.ss, i)
            nc.scalar.activation(squared[:, :], centered[:, :], ACT.Square, scale=D ** -0.5).then_inc(s.sq, 1)

        def norm_var(dve, s, i, squared, st):
            dve.wait_ge(s.sq, i + 1)
            nc.vector.tensor_reduce(st[:, 1, :], squared[:, :].rearrange("p (g d) -> p g d", d=D), AX.X,
                                    ALU.add).then_inc(s.ss, 1)

        def norm_std(act, s, i, st):
            act.wait_ge(s.ss, i + 1)
            nc.scalar.activation(st[:, 1, :], st[:, 1, :], ACT.Sqrt, bias=eps[:, 0:1]).then_inc(s.std, 1)

        def norm_rstd(dve, s, i, st):
            dve.wait_ge(s.std, i + 1)
            nc.vector.reciprocal(st[:, 2, :], st[:, 1, :]).then_inc(s.rstd, 1)

        def norm_relu(dve, s, i, centered, st, to, done=None):
            n = st.shape[2]
            dve.wait_ge(s.rstd, i + 1)
            nc.vector.scalar_tensor_tensor(out=to[:, :].rearrange("p (g d) -> p g d", d=D),
                                           in0=centered[:, :].rearrange("p (g d) -> p g d", d=D), scalar=0.0,
                                           in1=st[:, 2, :].unsqueeze(2).to_broadcast([P, n, D]),
                                           op0=ALU.max, op1=ALU.mult).then_inc(done or s.h, 1)

        def transposes(to, of, n, done):
            for j in range(n):
                last = nc.tensor.transpose(to[:, j * P:(j + 1) * P], of[:, j * P:(j + 1) * P], ident[:, :])
            last.then_inc(done, 1)

        def dst_columns(i, b):
            return nc.vector.tensor_copy(cols[b][:, :, :], dst_pair[:, bass.ds(i * Q, Q), :])

        def dst_rows(pe, s, i, b):
            pe.wait_ge(s.cols, i + 1)
            wait(pe, s.same, i)
            for q in range(Q):
                last = nc.tensor.transpose(psD[:, q * P:(q + 1) * P], cols[b][:, q, 0:1].to_broadcast([P, P]),
                                           ident[:, :])
            last.then_inc(s.dstb, 1)

        def dst_compare(dve, s, i, b):
            dve.wait_ge(s.dstb, i + 1)
            wait(dve, s.run_pe, Q * (i - 1))
            nc.vector.tensor_tensor(
                same[b][:, :, :, :],
                psD[:, :].rearrange("p (q o e) -> p q o e", q=Q, o=1).to_broadcast([P, Q, 2, P]),
                cols[b][:, :, :].unsqueeze(3).to_broadcast([P, Q, 2, P]), ALU.is_equal).then_inc(s.same, 1)

        def dst_sums(pe, s, i, b, tiles=range(Q)):
            pe.wait_ge(s.same, i + 1)
            pe.wait_ge(s.msg, i + 1)
            for q in tiles:
                to = psR[:, q * R1:(q + 1) * R1]
                before = run[b][:, q - 1, :] if q else run[1 - b][:, Q - 1, :]
                wait(pe, s.run, i * Q + q)
                nc.tensor.matmul(to, same[b][:, q, 0, :], msg[b][:, q, :], start=True, stop=False)
                nc.tensor.matmul(to, same[b][:, q, 1, :], before, start=False, stop=True).then_inc(s.run_pe, 1)

        def dst_sums_out(act, s, i, b, tiles):
            wait(act, s.rows, i - 1)
            for q in tiles:
                act.wait_ge(s.run_pe, i * Q + q + 1)
                nc.scalar.copy(run[b][:, q, :], psR[:, q * R1:(q + 1) * R1]).then_inc(s.run, 1)

        def dst_rows_out(dve, s, i, b, op, by):
            dve.wait_ge(s.run, (i + 1) * Q)
            nc.vector.tensor_scalar(rdeg[:, 0:Q], run[b][:, :, D], by, None, op).then_inc(s.deg, 1)
            dve.wait_ge(s.deg, i + 1)
            nc.vector.reciprocal(rdeg[:, Q:2 * Q], rdeg[:, 0:Q]).then_inc(s.rdeg, 1)
            dve.wait_ge(s.rdeg, i + 1)
            nc.vector.tensor_tensor(edge_rows[:, bass.ds(i * QD, QD)].rearrange("p (q d) -> p q d", d=D),
                                    run[b][:, :, 0:D], rdeg[:, Q:2 * Q].unsqueeze(2).to_broadcast([P, Q, D]),
                                    ALU.mult).then_inc(s.rows, 1)

        @block.gpsimd
        def _(pool):
            nc.gpsimd.memset(ident[:, :], 1.0).then_inc(pool_const, 1)
            nc.gpsimd.memset(sel[:, :], 1.0).then_inc(pool_const, 1)
            nc.gpsimd.iota(spare_i[:, :], [[P, T]], base=N, channel_multiplier=1).then_inc(pool_const, 1)
            nc.gpsimd.iota(bound_i[:, :], [[CHUNK, STEPS]], base=0, channel_multiplier=0).then_inc(pool_const, 1)
            pool.wait_ge(pool_const, 4)
            nc.gpsimd.affine_select(out=ident[:, :], in_=ident[:, :], pattern=[[-1, P]], compare_op=ALU.is_equal,
                                    fill=0.0, base=0, channel_multiplier=1).then_inc(pool_const, 1)
            nc.gpsimd.affine_select(out=sel[:, 0:1], in_=sel[:, 0:1], pattern=[[0, 1]], compare_op=ALU.is_equal,
                                    fill=0.0, base=1 - P, channel_multiplier=1).then_inc(pool_const, 1)

            def gather(table, j, landed):
                wait(pool, landed[j % UNROLL], 16 * Q * (j // UNROLL))
                for t in range(j * Q, (j + 1) * Q):
                    nc.gpsimd.indirect_dma_start(
                        out=edge_rows[:, t * D:(t + 1) * D], out_offset=None, in_=table,
                        in_offset=bass.IndirectOffsetOnAxis(ap=src_idx[:, t:t + 1], axis=0)
                    ).then_inc(landed[j % UNROLL], 16)

            def scatter(table, j, landed, op):
                wait(pool, landed[j % UNROLL], 16 * Q * (j // UNROLL))
                for t in range(j * Q, (j + 1) * Q):
                    nc.gpsimd.indirect_dma_start(
                        out=table, out_offset=bass.IndirectOffsetOnAxis(ap=end_idx[:, t:t + 1], axis=0),
                        in_=edge_rows[:, t * D:(t + 1) * D], in_offset=None, compute_op=op
                    ).then_inc(landed[j % UNROLL], 16)

            pool.wait_ge(idx_ready, 2)
            for j in range(STEPS):
                gather(x[:, :], j, a_gath)
            pool.wait_ge(spare_zeroed, 16 * SPARE_DMAS)
            pool.wait_ge(need_ready, 9)
            for j in range(STEPS):
                if j % UNROLL == 0:
                    last = min(j + UNROLL, STEPS) - 1
                    pool.wait_ge(x1_landed, pool.value_load(need[0:1, 0, last:last + 1], min_val=1, max_val=STEPS))
                    nc.gpsimd.nop(nofuse=True)
                pool.wait_ge(ae.rows, j + 1)
                scatter(x1_d[:, :], j, a_scat, ALU.add)
            for u in range(UNROLL):
                pool.wait_ge(a_scat[u], 16 * Q * ((STEPS - 1 - u) // UNROLL + 1))
            for j in range(STEPS):
                gather(x1_d[:, :], j, b_gath)
            pool.wait_ge(agg_zeroed, 16 * STEPS)
            for j in range(STEPS):
                pool.wait_ge(be.rows, j + 1)
                if j >= UNROLL:
                    pool.wait_ge(b_scat[j % UNROLL], 16 * Q * (j // UNROLL))
                    pool.sem_inc(agg_landed, 1)
                scatter(agg_d[:, :], j, b_scat, ALU.bypass)
            for j in range(STEPS - UNROLL, STEPS):
                pool.wait_ge(b_scat[j % UNROLL], 16 * Q * (j // UNROLL + 1))
                pool.sem_inc(agg_landed, 1)

        @block.vector
        def _(dve):
            for k, pad in enumerate((0, SENT, SENT)):
                nc.vector.memset(rows_i[k][:, :], pad).then_inc(filled, 1)
            for t, v in fills:
                nc.vector.memset(t[:], v).then_inc(filled, 1)
            nc.vector.memset(run[1][:, :, :], 0.0).then_inc(run_filled, 1)
            for k in range(2):
                nc.vector.memset(msg[k][:, :, D:R1], 1.0).then_inc(run_filled, 1)

            dve.wait_ge(bias_loaded, 32)
            for part in range(3):
                wait(dve, bias_split, 3 * part)
                nc.vector.tensor_copy(parts[:, :, part, :, :],
                                      (left if part else brow)[:, :, :].unsqueeze(2).to_broadcast([1, 2, NBLK, D])
                                      ).then_inc(bias_split, 1)
                if part < 2:
                    dve.wait_ge(bias_split, 3 * part + 1)
                    nc.vector.tensor_tensor(left[:, :, :], (left if part else brow)[:, :, :],
                                            parts[:, :, part, 0, :], ALU.subtract).then_inc(bias_split, 2)

            dve.wait_ge(rows_loaded, 16 * 9)
            for k in range(3):
                nc.vector.tensor_copy(rows_f[k][:, :], rows_i[k][:, :]).then_inc(rows_conv, 1)
            dve.wait_ge(pool_const, 6)
            nc.vector.tensor_copy(spare_f[:, :], spare_i[:, :]).then_inc(prep, 1)
            nc.vector.tensor_scalar(sel[:, 1:2], sel[:, 0:1], 1.0, None, ALU.subtract).then_inc(prep, 1)
            dve.wait_ge(idxT, 1)
            nc.vector.tensor_copy(src_idx[:, :], psH[:, 0:T]).then_inc(idx_ready, 1)
            dve.wait_ge(idxT, 2)
            nc.vector.tensor_copy(dst_f[:, :], psE[:, 0:T]).then_inc(prep, 1)
            nc.vector.tensor_copy(dst_pair[:, :, 0], psE[:, 0:T]).then_inc(prep, 1)
            dve.wait_ge(idxT, 3)
            nc.vector.tensor_copy(next_f[:, :], psR[:, 0:T]).then_inc(prep, 1)
            nc.vector.memset(dst_pair[:, 0:1, 1], -1.0).then_inc(prep, 1)
            dve.wait_ge(prep, 6)
            nc.vector.tensor_scalar(dst_pair[:, 1:T, 1], dst_f[:, 0:T - 1], sel[:, 0:1], sel[:, 1:2],
                                    ALU.mult, ALU.add).then_inc(prep, 1)
            dve.wait_ge(prep, 7)
            nc.vector.tensor_tensor(next_f[:, :], next_f[:, :], dst_f[:, :], ALU.not_equal).then_inc(prep, 1)
            nc.vector.tensor_tensor(dst_f[:, :], dst_f[:, :], spare_f[:, :], ALU.subtract).then_inc(prep, 1)
            dve.wait_ge(prep, 9)
            nc.vector.tensor_tensor(dst_f[:, :], dst_f[:, :], next_f[:, :], ALU.mult).then_inc(prep, 1)
            dve.wait_ge(prep, 10)
            nc.vector.tensor_tensor(end_idx[:, :], dst_f[:, :], spare_f[:, :], ALU.add).then_inc(idx_ready, 1)

            nc.vector.tensor_copy(first_f[:, 0:STEPS], dst_pair[0:1, 0:T:Q, 0]).then_inc(need_ready, 1)
            nc.vector.memset(first_f[:, STEPS:STEPS + 1], SENT).then_inc(need_ready, 1)
            nc.vector.tensor_copy(bound_f[:, :], bound_i[:, :]).then_inc(need_ready, 1)
            dve.wait_ge(need_ready, 3)
            nc.vector.tensor_tensor(less[:, :, :], bound_f[:, :].unsqueeze(1).to_broadcast([1, STEPS, STEPS]),
                                    first_f[:, 1:STEPS + 1].unsqueeze(2).to_broadcast([1, STEPS, STEPS]),
                                    ALU.is_le).then_inc(need_ready, 1)
            dve.wait_ge(need_ready, 4)
            nc.vector.tensor_reduce(need_f[:, 0, :], less[:, :, :], AX.X, ALU.add).then_inc(need_ready, 1)
            nc.vector.tensor_scalar(bound_f[:, :], bound_f[:, :], float(CHUNK), None, ALU.add
                                    ).then_inc(need_ready, 1)
            dve.wait_ge(need_ready, 6)
            nc.vector.tensor_tensor(less[:, :, :], first_f[:, 0:STEPS].unsqueeze(1).to_broadcast([1, STEPS, STEPS]),
                                    bound_f[:, :].unsqueeze(2).to_broadcast([1, STEPS, STEPS]),
                                    ALU.is_lt).then_inc(need_ready, 1)
            dve.wait_ge(need_ready, 7)
            nc.vector.tensor_reduce(need_f[:, 1, :], less[:, :, :], AX.X, ALU.add).then_inc(need_ready, 1)
            dve.wait_ge(need_ready, 8)
            nc.vector.tensor_scalar(need[:, :, :], need_f[:, :, :], 1.0, None, ALU.max).then_inc(need_ready, 1)

            dve.wait_ge(w_loaded, 16 * W_DMAS)
            nc.vector.tensor_tensor(b2sum[:, :], b2c[:, 0:1].to_broadcast([D, P]), b2c[:, 1:2].to_broadcast([D, P]),
                                    ALU.add).then_inc(w_prep, 1)
            dve.wait_ge(w_pe, 1)
            nc.vector.tensor_copy(w_bd[:, :, :], psT[0][:, 0:2 * P].rearrange("p (a c) -> p a c", a=2)
                                  ).then_inc(w_prep, 1)
            nc.vector.tensor_copy(w2t[:, :], psT[1][0:D, 0:P]).then_inc(w_prep, 1)
            dve.wait_ge(w_pe, 2)
            nc.vector.tensor_copy(w2u[:, :], psY[:, 0:D]).then_inc(w_prep, 1)
            nc.vector.tensor_copy(b2u[:, :, :], psY[0:1, D:2 * D].unsqueeze(1).to_broadcast([1, Q, D])
                                  ).then_inc(w_prep, 1)

            def edge_view(i):
                return edge_rows[:, bass.ds(i * QD, QD)].rearrange("p (q d) -> p q d", d=D)

            def node_view(u):
                return xin[u][:, :].rearrange("p (g d) -> p g d", d=D)

            def sums_a(i, k, u):
                if real(i):
                    dve.wait_ge(a_x[u], 16 * (k + 1))
                    norm_sum(dve, ad, i, node_view(u), stat)
                    dve.wait_ge(a_gath[u], 16 * Q * (k + 1))
                    norm_sum(dve, ae, i, edge_view(i), state)

            def center_a(i, u):
                if real(i):
                    norm_center(dve, ad, i, node_view(u), stat, xc[u % 2])
                    norm_center(dve, ae, i, edge_view(i), state, xce[u % 2])

            def columns(s, i, b):
                if real(i):
                    dst_columns(i, b).then_inc(s.cols, 1)

            columns(ae, 0, 0)
            sums_a(0, 0, 0)
            center_a(0, 0)
            sums_a(1, 0, 1)

            def step_a(i, k, u):
                b = u % 2
                norm_var(dve, ad, i, sq, stat)
                norm_var(dve, ae, i, sqe, state)
                center_a(i + 1, (u + 1) % UNROLL)
                dst_compare(dve, ae, i, b)
                columns(ae, i + 1, 1 - b)
                norm_rstd(dve, ae, i, stats)
                wait(dve, ad.tr1, i - 1)
                norm_relu(dve, ae, i, xc[b], stat, h[b], ad.h)
                wait(dve, ae.tr, i - 1)
                norm_relu(dve, ae, i, xce[b], state, he[b])
                sums_a(i + 2, k + (u + 2) // UNROLL, (u + 2) % UNROLL)
                if real(i - 2):
                    dst_rows_out(dve, ae, i - 2, b, ALU.max, 1.0)

            steps(dve, step_a)
            dst_rows_out(dve, ae, STEPS - 2, 1, ALU.max, 1.0)
            dst_rows_out(dve, ae, STEPS - 1, 0, ALU.max, 1.0)

            def sums_be(i, k, u):
                if real(i):
                    dve.wait_ge(b_gath[u], 16 * Q * (k + 1))
                    norm_sum(dve, be, i, edge_view(i), state)

            def center_be(i, b):
                if real(i):
                    norm_center(dve, be, i, edge_view(i), state, xce[b])

            columns(be, 0, 0)
            sums_be(0, 0, 0)
            center_be(0, 0)
            sums_be(1, 0, 1)

            def step_be(i, k, u):
                b = u % 2
                norm_var(dve, be, i, sqe, state)
                center_be(i + 1, 1 - b)
                norm_rstd(dve, be, i, state)
                dst_compare(dve, be, i, b)
                columns(be, i + 1, 1 - b)
                wait(dve, be.tr, i - 1)
                norm_relu(dve, be, i, xce[b], state, he[b])
                sums_be(i + 2, k + (u + 2) // UNROLL, (u + 2) % UNROLL)
                if real(i - 2):
                    dst_rows_out(dve, be, i - 2, b, ALU.add, 1e-8)

            steps(dve, step_be)
            dst_rows_out(dve, be, STEPS - 2, 1, ALU.add, 1e-8)
            dst_rows_out(dve, be, STEPS - 1, 0, ALU.add, 1e-8)

            def sums_bd(i, k, u):
                if real(i):
                    dve.wait_ge(b_x[u], 16 * (k + 1))
                    norm_sum(dve, bd, i, node_view(u), stat)

            def center_bd(i, u):
                if real(i):
                    norm_center(dve, bd, i, node_view(u), stat, xc[u % 2])

            def finish_bd(i, u):
                if real(i):
                    dve.wait_ge(bd.y1, i + 1)
                    nc.vector.tensor_tensor(xin[u][:, :], psY[:, :], xin[u][:, :], ALU.add).then_inc(bd.out, 1)

            sums_bd(0, 0, 0)
            center_bd(0, 0)
            sums_bd(1, 0, 1)

            def step_bd(i, k, u):
                norm_var(dve, bd, i, sq, stat)
                center_bd(i + 1, (u + 1) % UNROLL)
                norm_rstd(dve, bd, i, stat)
                wait(dve, bd.tr1, i - 1)
                norm_relu(dve, bd, i, xc[u % 2], stat, h[u % 2])
                sums_bd(i + 2, k + (u + 2) // UNROLL, (u + 2) % UNROLL)
                finish_bd(i - 1, (u - 1) % UNROLL)

            steps(dve, step_bd)
            finish_bd(STEPS - 1, 0)

        @block.scalar
        def _(act):
            def node_square(s, i, b):
                if real(i):
                    norm_square(act, s, i, xc[b], sq)

            def edge_square(s, i, b):
                if real(i):
                    norm_square(act, s, i, xce[b], sqe)

            def transposed_out(s, i, b, half):
                act.wait_ge((s.tr0, s.tr1)[half], i + 1)
                nc.scalar.copy(hT[b][:, half * 512:(half + 1) * 512], psT[half][:, :]
                               ).then_inc((s.hT0, s.hT1)[half], 1)

            def x1_out(i, u, half):
                if real(i):
                    act.wait_ge((ad.y0, ad.y1)[half], i + 1)
                    nc.scalar.copy(xin[u][:, half * 512:(half + 1) * 512], psY[:, half * 512:(half + 1) * 512]
                                   ).then_inc((ad.x1_0, ad.x1)[half], 1)

            def msg_a(i, b):
                act.wait_ge(ae.w, i + 1)
                wait(act, ae.run_pe, Q * (i - 1))
                if isinstance(i, int) and i < 2:
                    act.wait_ge(run_filled, RUN_FILLED)
                nc.scalar.copy(msg[b][:, :, 0:D], psH[:, 0:QD].rearrange("p (q d) -> p q d", d=D)
                               ).then_inc(ae.msg, 1)

            node_square(ad, 0, 0)
            edge_square(ae, 0, 0)

            def step_a(i, k, u):
                b = u % 2
                act.wait_ge(ad.ss, i + 1)
                norm_std(act, ae, i, stats)
                node_square(ad, i + 1, 1 - b)
                edge_square(ae, i + 1, 1 - b)
                if real(i - 1):
                    dst_sums_out(act, ae, i - 1, 1 - b, range(0, 2))
                    x1_out(i - 1, (u - 1) % UNROLL, 0)
                    dst_sums_out(act, ae, i - 1, 1 - b, range(2, Q))
                    x1_out(i - 1, (u - 1) % UNROLL, 1)
                wait(act, ad.y1, i - 1)
                transposed_out(ad, i, b, 0)
                act.wait_ge(ae.tr, i + 1)
                wait(act, ae.w, i - 1)
                nc.scalar.copy(hTe[b][:, :], psE[:, 0:QD]).then_inc(ae.hT, 1)
                transposed_out(ad, i, b, 1)
                msg_a(i, b)

            steps(act, step_a)
            dst_sums_out(act, ae, STEPS - 1, 0, range(Q))
            for half in range(2):
                x1_out(STEPS - 1, 0, half)

            edge_square(be, 0, 0)

            def step_be(i, k, u):
                b = u % 2
                norm_std(act, be, i, state)
                edge_square(be, i + 1, 1 - b)
                if real(i - 1):
                    dst_sums_out(act, be, i - 1, 1 - b, range(Q))
                act.wait_ge(be.eatr, i + 1)
                wait(act, be.hid_pe, i - 1)
                nc.scalar.copy(hTe[b][:, :], psE[:, 0:QD]).then_inc(be.hT, 1)
                nc.scalar.copy(eaT[b][:, :], psE[:, QD:QD + P]).then_inc(be.eaT, 1)
                act.wait_ge(be.hid_pe, i + 1)
                wait(act, be.w, i - 1)
                nc.scalar.activation(hid[b][:, :], psH[:, :], ACT.Relu, bias=b1c[:, 0:1]).then_inc(be.hid, 1)
                act.wait_ge(be.w, i + 1)
                wait(act, be.run_pe, Q * (i - 1))
                nc.scalar.copy(msg[b][:, :, 0:D], psY[:, 0:QD].rearrange("p (q d) -> p q d", d=D)
                               ).then_inc(be.msg, 1)

            steps(act, step_be)
            dst_sums_out(act, be, STEPS - 1, 0, range(Q))

            node_square(bd, 0, 0)

            def step_bd(i, k, u):
                b = u % 2
                norm_std(act, bd, i, stat)
                node_square(bd, i + 1, 1 - b)
                wait(act, bd.p1, i - 1)
                for half in range(2):
                    transposed_out(bd, i, b, half)
                for half in range(2):
                    act.wait_ge((bd.p0, bd.p1)[half], i + 1)
                    wait(act, (bd.y0, bd.y1)[half], i)
                    nc.scalar.activation(hid[half][:, :], psP[half][:, :], ACT.Relu, bias=ub1c[:, 0:1]
                                         ).then_inc((bd.r0, bd.r1)[half], 1)

            steps(act, step_bd)

        @block.tensor
        def _(pe):
            pe.wait_ge(pool_const, 6)
            for k, to in enumerate((psH, psE, psR)):
                pe.wait_ge(rows_conv, k + 1)
                for a in range(2):
                    last = nc.tensor.transpose(to[:, a * H:(a + 1) * H], rows_f[k][:, a * P:(a + 1) * P],
                                               ident[0:H, 0:H])
                last.then_inc(idxT, 1)
            pe.wait_ge(w_loaded, 16 * W_DMAS)
            for half in range(2):
                nc.tensor.transpose(psT[0][:, half * P:(half + 1) * P], w_raw[:, half, :], ident[:, :])
            nc.tensor.transpose(psT[1][0:D, 0:P], w2[:, :], ident[:, :]).then_inc(w_pe, 1)
            pe.wait_ge(w_prep, 3)
            nc.tensor.matmul(psY[:, 0:D], w2t[:, :], u1b[:, :], start=True, stop=True)
            nc.tensor.matmul(psY[:, D:2 * D], b2sum[:, :], u1b[:, :], start=True, stop=True).then_inc(w_pe, 1)
            pe.wait_ge(w_prep, 5)
            pe.wait_ge(idx_ready, 2)

            def norm_transposes(s, i, b):
                pe.wait_ge(s.h, i + 1)
                for half in range(2):
                    wait(pe, (s.hT0, s.hT1)[half], i)
                    transposes(psT[half], h[b][:, half * 512:(half + 1) * 512], 4, (s.tr0, s.tr1)[half])

            def by_nodes(s, i, half, source, weights, bias, ready, done, read, add=None):
                to = psY[:, half * 512:(half + 1) * 512]
                wait(pe, read, i)
                nc.tensor.matmul(to, ones3[:, :], bias3[:, bias, :], start=True, stop=False)
                if add is not None:
                    nc.tensor.matmul(to, ident[:, :], add[:, half * 512:(half + 1) * 512], start=False, stop=False)
                pe.wait_ge(ready, i + 1)
                for j in range(4):
                    last = nc.tensor.matmul(to[:, j * P:(j + 1) * P], source[:, j * P:(j + 1) * P], weights,
                                            start=False, stop=j == 3)
                last.then_inc(done, 1)

            pe.wait_ge(bias_moved, 16 * 6)
            dst_rows(pe, ae, 0, 0)

            def step_a(i, k, u):
                b = u % 2
                norm_transposes(ad, i, b)
                pe.wait_ge(ae.h, i + 1)
                wait(pe, ae.hT, i)
                transposes(psE[:, 0:QD], he[b], 2, ae.tr)
                if real(i + 1):
                    dst_rows(pe, ae, i + 1, 1 - b)
                pe.wait_ge(ae.hT, i + 1)
                wait(pe, ae.msg, i)
                for j in range(2):
                    last = nc.tensor.matmul(psH[:, j * P:(j + 1) * P], hTe[b][:, j * P:(j + 1) * P],
                                            w_bd[:, 1, :], start=True, stop=True)
                last.then_inc(ae.w, 1)
                for half in range(2):
                    by_nodes(ad, i, half, hT[b][:, half * 512:(half + 1) * 512], w_bd[:, 0, :], 0,
                             (ad.hT0, ad.hT1)[half], (ad.y0, ad.y1)[half], (ad.x1_0, ad.x1)[half], xin[u])
                    dst_sums(pe, ae, i, b, range(2 * half, 2 * half + 2))

            steps(pe, step_a)
            dst_rows(pe, be, 0, 0)

            def step_be(i, k, u):
                b = u % 2
                pe.wait_ge(be.h, i + 1)
                wait(pe, be.eaT, i)
                transposes(psE[:, 0:QD], he[b], 2, be.tr)
                pe.wait_ge(b_ea[u], 16 * (k + 1) if not (isinstance(i, int) and i == STEPS - 1) else 16 * (k + 2))
                transposes(psE[:, QD:QD + P], ea[u], 1, be.eatr)
                if real(i + 1):
                    dst_rows(pe, be, i + 1, 1 - b)
                pe.wait_ge(be.hT, i + 1)
                wait(pe, be.hid, i)
                for a in range(2):
                    nc.tensor.matmul(psH[:, a * QD:(a + 1) * QD], w1h[:, a, :], hTe[b][:, :], start=a == 0,
                                     stop=False)
                pe.wait_ge(be.eaT, i + 1)
                for q in range(Q):
                    at = ((q % 2) * 2 + q // 2) * P
                    last = nc.tensor.matmul(psH[:, at:at + P], w1e[:, q, :], eaT[b][:, :], start=False,
                                            stop=q == Q - 1)
                last.then_inc(be.hid_pe, 1)
                wait(pe, be.msg, i)
                nc.tensor.matmul(psY[:, 0:QD], ones[0:1, :], b2u[0:1, :, :], start=True, stop=False)
                pe.wait_ge(be.hid, i + 1)
                for q in range(Q):
                    at = ((q % 2) * 2 + q // 2) * P
                    last = nc.tensor.matmul(psY[:, q * D:(q + 1) * D], hid[b][:, at:at + P], w2u[:, :],
                                            start=False, stop=q == Q - 1)
                last.then_inc(be.w, 1)
                dst_sums(pe, be, i, b)

            steps(pe, step_be)

            def step_bd(i, k, u):
                b = u % 2
                norm_transposes(bd, i, b)
                pe.wait_ge(b_agg[b], 16 * (k * 2 + u // 2 + 1))
                for half in range(2):
                    pe.wait_ge((bd.hT0, bd.hT1)[half], i + 1)
                    wait(pe, (bd.r0, bd.r1)[half], i)
                    nc.tensor.matmul(psP[half][:, :], u1_bd[:, :], hT[b][:, half * 512:(half + 1) * 512],
                                     start=True, stop=False)
                    for j in range(4):
                        at = half * 512 + j * P
                        last = nc.tensor.matmul(psP[half][:, j * P:(j + 1) * P], agg[b][:, at:at + P],
                                                ident[:, :], start=False, stop=j == 3)
                    last.then_inc((bd.p0, bd.p1)[half], 1)
                for half in range(2):
                    by_nodes(bd, i, half, hid[half], u2_bd[:, :], 1, (bd.r0, bd.r1)[half],
                             (bd.y0, bd.y1)[half], bd.out)

            steps(pe, step_bd)


_INS = ['x', 'src', 'dst', 'edge_attr_32', 'L0_gnn_W', 'L0_gnn_b', 'L1_gnn_msg_w1', 'L1_gnn_msg_b1',
        'L1_gnn_msg_w2', 'L1_gnn_msg_b2', 'L1_gnn_upd_w1', 'L1_gnn_upd_b1', 'L1_gnn_upd_w2', 'L1_gnn_upd_b2']


def kernel(**inputs):
    import numpy as _np
    import concourse.bacc as _bacc
    from concourse import mybir as _mybir
    from concourse.bass_utils import run_bass_kernel_spmd as _run

    nc = _bacc.Bacc("TRN2", target_bir_lowering=False, num_devices=1)
    arrays, args = {}, []
    for name in _INS:
        a = _np.ascontiguousarray(inputs[name])
        arrays[f"in_{name}"] = a
        args.append(nc.dram_tensor(f"in_{name}", a.shape, _mybir.dt.from_np(a.dtype), kind="ExternalInput").ap())
    shape = inputs['x'].shape
    args.append(nc.dram_tensor("out", shape, _mybir.dt.float32, kind="ExternalOutput").ap())
    gnn_program(nc, *args)
    r = _run(nc, [arrays], core_ids=[0])
    return r.results[0]["out"]
```

```python
import concourse.bass as bass
from concourse import mybir
from collections import namedtuple
from contextlib import ExitStack

FP32 = mybir.dt.float32
I32 = mybir.dt.int32
BF16 = mybir.dt.bfloat16
ALU = mybir.AluOpType
ACT = mybir.ActivationFunctionType
AX = mybir.AxisListType


def gnn_program(nc, x, src, dst, edge_attr, gnn_w, gnn_b, msg_w1, msg_b1, msg_w2, msg_b2,
                upd_w1, upd_b1, upd_w2, upd_b2, out):
    N, D = x.shape
    E = src.shape[0]
    DE = edge_attr.shape[1]
    P = 128
    G = 16
    CHUNK = P * G
    NFULL = N // CHUNK
    STEPS = NFULL + 1
    PREST = (N - NFULL * CHUNK) // G
    assert PREST * G + NFULL * CHUNK == N
    Q = 4
    T = STEPS * Q
    assert (T - Q) * P < E <= T * P
    EPAD = T * P
    TF = E // P
    EREST = E - TF * P
    H = T // 2
    UNROLL = 4
    assert STEPS % UNROLL == 1
    GD = G * D
    QD = Q * D
    C = D + DE
    NBLK = GD // P
    R1 = D + 1
    EPS = 1e-5
    SENT = 1 << 17

    x1_d = nc.dram_tensor("x1_scratch", (N + EPAD, D), FP32, kind="Internal").ap()
    agg_d = nc.dram_tensor("agg_scratch", (N + EPAD, D), FP32, kind="Internal").ap()

    ctx = ExitStack()
    with ctx:
        def sb(name, shape, dt=FP32):
            return ctx.enter_context(nc.sbuf_tensor(name, shape, dt))

        def pb(name, cols):
            return ctx.enter_context(nc.psum_tensor(name, [P, cols], FP32))

        def sem(name):
            return ctx.enter_context(nc.semaphore(name))

        def sems(name, n):
            return [sem(f"{name}{k}") for k in range(n)]

        ident = sb("ident", [P, P])
        zeros = sb("zeros", [P, GD])
        ones = sb("ones", [1, P])
        ones3 = sb("ones3", [3, P], BF16)
        sel = sb("sel", [P, 2])
        rows_i = [sb(f"rows_i{k}", [H, 2 * P], I32) for k in range(3)]
        rows_f = [sb(f"rows_f{k}", [H, 2 * P]) for k in range(3)]
        src_idx = sb("src_idx", [P, T], I32)
        end_idx = sb("end_idx", [P, T], I32)
        dst_f = sb("dst_f", [P, T])
        next_f = sb("next_f", [P, T])
        spare_f = sb("spare_f", [P, T])
        spare_i = sb("spare_i", [P, T], I32)
        dst_pair = sb("dst_pair", [P, T, 2])
        w_raw = sb("w_raw", [P, 2, P])
        w_bd = sb("w_bd", [P, 2, P])
        u1_bd = sb("u1_bd", [P, P])
        u2_bd = sb("u2_bd", [P, P])
        w1 = sb("w1", [C, P])
        w2 = sb("w2", [P, D])
        w2t = sb("w2t", [D, P])
        u1b = sb("u1b", [D, D])
        w2u = sb("w2u", [P, D])
        b2c = sb("b2c", [D, 2])
        b2sum = sb("b2sum", [D, P])
        b2u = sb("b2u", [1, 2, D])
        b2u_parts = sb("b2u_parts", [1, 3, Q, D], BF16)
        b2u3 = sb("b2u3", [3, QD], BF16)
        b1c = sb("b1c", [P, 1])
        ub1c = sb("ub1c", [P, 1])
        brow = sb("brow", [1, 2, D])
        left = sb("left", [1, 2, D])
        parts = sb("parts", [1, 2, 3, NBLK, D], BF16)
        bias3 = sb("bias3", [3, 2, NBLK * D], BF16)
        first_i = sb("first_i", [1, STEPS + 1], I32)
        first_f = sb("first_f", [1, STEPS])
        chunk_i = sb("chunk_i", [1, STEPS], I32)
        bound_i = sb("bound_i", [1, STEPS], I32)
        bound_f = sb("bound_f", [1, STEPS])
        less = sb("less", [1, STEPS, STEPS])
        need_f = sb("need_f", [1, STEPS])
        need = sb("need", [1, 2, STEPS], I32)

        edge_rows = sb("edge_rows", [P, T * D])
        xin = [sb(f"xin{k}", [P, GD]) for k in range(UNROLL)]
        agg = [sb(f"agg{k}", [P, GD]) for k in range(2)]
        xc = [sb(f"xc{k}", [P, GD]) for k in range(2)]
        sq = sb("sq", [P, GD])
        h = [sb(f"h{k}", [P, GD]) for k in range(2)]
        hT = [sb(f"hT{k}", [P, GD]) for k in range(2)]
        xce = [sb(f"xce{k}", [P, QD]) for k in range(2)]
        sqe = sb("sqe", [P, QD])
        he = [sb(f"he{k}", [P, QD]) for k in range(2)]
        hTe = [sb(f"hTe{k}", [P, QD]) for k in range(2)]
        stats = sb("stats", [P, 3, G + Q])
        stat = stats[:, :, 0:G]
        state = stats[:, :, G:G + Q]
        eps = sb("eps", [P, 1])
        cols = [sb(f"cols{k}", [P, Q, 2]) for k in range(2)]
        same = [sb(f"same{k}", [P, Q, 2, P]) for k in range(UNROLL)]
        msg = [sb(f"msg{k}", [P, Q, R1]) for k in range(2)]
        run = [sb(f"run{k}", [P, Q, R1]) for k in range(2)]
        rdeg = sb("rdeg", [P, 2 * Q])
        comb = [sb(f"comb{k}", [P, Q, C]) for k in range(UNROLL)]
        res = [sb(f"res{k}", [P, GD]) for k in range(2)]
        hid = [sb(f"hid{k}", [P, Q * P]) for k in range(2)]

        psD = pb("psD", 512)
        psT = [pb(f"psT{k}", 512) for k in range(2)]
        psY = pb("psY", 1024)
        psE = pb("psE", 512)
        psR = pb("psR", 512)
        psH = pb("psH", 512)

        def wait(eng, s, value):
            if not isinstance(value, int) or value > 0:
                eng.wait_ge(s, value)

        def real(i):
            return not isinstance(i, int) or 0 <= i < STEPS

        def step(body, i):
            body(i, i // UNROLL, i % UNROLL)

        def steps(eng, body, peel=2, lead=0, lag=0):
            turns = STEPS // UNROLL
            for i in range(-lead, 0):
                step(body, i)
            for u in range(UNROLL):
                body(u, 0, u)
            with eng.Fori(1, turns + 1 - peel) as k:
                for u in range(UNROLL):
                    body(k * UNROLL + u, k, u)
            for k in range(turns + 1 - peel, turns):
                for u in range(UNROLL):
                    body(k * UNROLL + u, k, u)
            for i in range(STEPS - 1, STEPS + lag):
                step(body, i)

        psP = [psD, psH]

        wa_loaded = sem("wa_loaded")
        wb_loaded = sem("wb_loaded")
        rows_loaded = sems("rows_loaded", 3)
        filled = sem("filled")
        pool_const = sem("pool_const")
        rows_conv = sem("rows_conv")
        idxT = sem("idxT")
        prep = sem("prep")
        w_prep = sem("w_prep")
        w_pe = sem("w_pe")
        bias_loaded = sem("bias_loaded")
        bias_split = sem("bias_split")
        bias_moved = sem("bias_moved")
        b2u_split = sem("b2u_split")
        b2u_moved = sem("b2u_moved")
        need0_ready = sem("need0_ready")
        need1_ready = sem("need1_ready")
        x1_landed = sem("x1_landed")
        agg_landed = sem("agg_landed")
        run_filled = sem("run_filled")
        idx_ready = sem("idx_ready")
        agg_zeroed = sem("agg_zeroed")

        a_x = sems("a_x", UNROLL)
        a_gath = sems("a_gath", UNROLL)
        a_stored = sems("a_stored", UNROLL)
        a_spare = sems("a_spare", UNROLL)
        a_scat = sems("a_scat", UNROLL)
        b_x = sems("b_x", UNROLL)
        b_agg = sems("b_agg", 2)
        b_gath = sems("b_gath", UNROLL)
        b_ea = sems("b_ea", UNROLL)
        b_scat = sems("b_scat", UNROLL)
        b_stored = sems("b_stored", UNROLL)

        def stage(prefix, names):
            return namedtuple(prefix, names)(*(sem(f"{prefix}_{n}") for n in names))

        LN = ["sum", "xc", "sq", "ss", "std", "rstd", "h"]
        SEG = ["cols", "dstb", "same", "msg", "run_pe", "run", "deg", "rdeg", "rows"]
        ad = stage("ad", LN + ["tr0", "tr1", "hT0", "hT1", "y0", "y1", "x1_0", "x1"])
        ae = stage("ae", LN + SEG + ["tr", "hT", "w"])
        bd = stage("bd", LN + ["tr0", "tr1", "hT0", "hT1", "p0", "p1", "r0", "r1", "y0", "y1", "out0", "out"])
        be = stage("be", LN + SEG + ["tr", "hT", "hid_pe", "hid", "w"])

        fills = [(zeros, 0.0), (u1_bd, 0.0), (u2_bd, 0.0), (ones, 1.0), (eps, EPS), (ones3, 1.0)]
        FILLED_W = 4
        FILLED_ALL = FILLED_W + len(fills)
        RUN_FILLED = 3
        WA_DMAS = 4
        WB_DMAS = 2 * (2 + 1 + 2) + 3

        block = ctx.enter_context(nc.Block())

        def node_chunk(t, i):
            return t[bass.ds(i * CHUNK, CHUNK), :].rearrange("(p g) d -> p (g d)", p=P)

        def node_rest(t):
            return t[NFULL * CHUNK:N, :].rearrange("(p g) d -> p (g d)", p=PREST)

        @block.sync
        def _(sp):
            def load_rows(k, v, first):
                n = E - first
                full = n // P
                rest = n - full * P
                sp.wait_ge(filled, k + 1)
                sp.dma_start(rows_i[k][:, 0:P], v[first:first + H * P].rearrange("(q c) -> q c", c=P)
                             ).then_inc(rows_loaded[k], 16)
                sp.dma_start(rows_i[k][0:full - H, P:2 * P],
                             v[first + H * P:first + full * P].rearrange("(q c) -> q c", c=P)
                             ).then_inc(rows_loaded[k], 16)
                sp.dma_start(rows_i[k][full - H:full - H + 1, P:P + rest],
                             v[first + full * P:first + n].rearrange("(q c) -> q c", q=1)
                             ).then_inc(rows_loaded[k], 16)

            def load_layer2():
                sp.wait_ge(filled, FILLED_ALL)
                for a in range(2):
                    lo = a * D
                    sp.dma_start(u1_bd[lo:lo + D, lo:lo + D], upd_w1[0:D, :]).then_inc(wb_loaded, 16)
                    sp.dma_start(u2_bd[lo:lo + D, lo:lo + D], upd_w2[:, :]).then_inc(wb_loaded, 16)
                    sp.dma_start(w1[:, lo:lo + D], msg_w1[a, :, :]).then_inc(wb_loaded, 16)
                    sp.dma_start(ub1c[lo:lo + D, :], upd_b1.rearrange("(f o) -> f o", o=1)).then_inc(wb_loaded, 16)
                    sp.dma_start(b2c[:, a:a + 1], msg_b2[a, :].rearrange("(f o) -> f o", o=1)
                                 ).then_inc(wb_loaded, 16)
                sp.dma_start(w2[:, :], msg_w2.rearrange("l f o -> (l f) o")).then_inc(wb_loaded, 16)
                sp.dma_start(u1b[:, :], upd_w1[D:2 * D, :]).then_inc(wb_loaded, 16)
                sp.dma_start(b1c[:, :], msg_b1.rearrange("l (f o) -> (l f) o", o=1)).then_inc(wb_loaded, 16)

            def load_x(t, i, k, u, landed):
                if isinstance(i, int) and i == STEPS - 1:
                    sp.dma_start(xin[u][0:PREST, :], node_rest(t)).then_inc(landed[u], 16)
                else:
                    sp.dma_start(xin[u][:, :], node_chunk(t, i)).then_inc(landed[u], 16)

            def store_x(of, t, i, u, stored):
                if isinstance(i, int) and i == STEPS - 1:
                    sp.dma_start(node_rest(t), of[0:PREST, :]).then_inc(stored[u], 16)
                else:
                    sp.dma_start(node_chunk(t, i), of[:, :]).then_inc(stored[u], 16)

            load_rows(0, src, 0)
            load_x(x, 0, 0, 0, a_x)
            sp.wait_ge(filled, FILLED_W)
            for a in range(2):
                lo = a * D
                for half in range(2):
                    sp.dma_start(w_raw[lo:lo + D, half, lo:lo + D], gnn_w[:, half * D:(half + 1) * D]
                                 ).then_inc(wa_loaded, 16)
            sp.dma_start(brow[:, 0, :], gnn_b.rearrange("(o f) -> o f", o=1)).then_inc(bias_loaded, 16)
            sp.dma_start(brow[:, 1, :], upd_b2.rearrange("(o f) -> o f", o=1)).then_inc(bias_loaded, 16)
            load_rows(1, dst, 0)
            load_rows(2, dst, 1)
            load_x(x, 1, 0, 1, a_x)
            load_x(x, 2, 0, 2, a_x)
            sp.wait_ge(bias_split, 7)
            for n in range(2):
                for part in range(3):
                    sp.dma_start(bias3[part:part + 1, n, :], parts[0:1, n, part, :, :].rearrange("p a d -> p (a d)")
                                 ).then_inc(bias_moved, 16)

            def step_a(i, k, u):
                if real(i):
                    if real(i + 3):
                        wait(sp, ad.y1, i)
                        load_x(x, i + 3, k + (u + 3) // UNROLL, (u + 3) % UNROLL, a_x)
                    if isinstance(i, int) and i == 0:
                        sp.wait_ge(filled, FILLED_ALL)
                    if isinstance(i, int) and i == STEPS - 1:
                        sp.dma_start(node_rest(agg_d), zeros[0:PREST, :]).then_inc(agg_zeroed, 16)
                    else:
                        sp.dma_start(node_chunk(agg_d, i), zeros[:, :]).then_inc(agg_zeroed, 16)
                    sp.dma_start(x1_d[bass.ds(N + i * (Q * P), Q * P), :].rearrange("(p q) d -> p (q d)", p=P),
                                 zeros[:, 0:QD]).then_inc(a_spare[u], 16)
                if real(i - 2):
                    sp.wait_ge(a_spare[(u + 2) % UNROLL], 16 * (k + (u - 2) // UNROLL + 1))
                    sp.wait_ge(a_stored[(u + 2) % UNROLL], 16 * (k + (u - 2) // UNROLL + 1))
                    sp.sem_inc(x1_landed, 1)
                if real(i - 1):
                    sp.wait_ge(ad.x1, i)
                    store_x(res[(u + 1) % 2], x1_d, i - 1, (u - 1) % UNROLL, a_stored)
                if isinstance(i, int) and i == 2:
                    load_layer2()

            steps(sp, step_a, lag=2)

            sp.wait_ge(b2u_split, 5)
            for part in range(3):
                sp.dma_start(b2u3[part:part + 1, :], b2u_parts[0:1, part, :, :].rearrange("p q d -> p (q d)")
                             ).then_inc(b2u_moved, 16)
            for u in range(UNROLL):
                sp.wait_ge(a_scat[u], 16 * Q * ((STEPS - 1 - u) // UNROLL + 1))
            def step_ea(i, k, u):
                wait(sp, be.tr, i - UNROLL + 1)
                if isinstance(i, int) and i == STEPS - 1:
                    e0 = i * Q * P
                    nf = TF - i * Q
                    sp.dma_start(comb[u][:, 0:nf, D:C], edge_attr[e0:e0 + nf * P, :].rearrange("(q p) c -> p q c", p=P)
                                 ).then_inc(b_ea[u], 16)
                    sp.dma_start(comb[u][0:EREST, nf, D:C], edge_attr[e0 + nf * P:E, :]).then_inc(b_ea[u], 16)
                else:
                    sp.dma_start(comb[u][:, :, D:C],
                                 edge_attr[bass.ds(i * (Q * P), Q * P), :].rearrange("(q p) c -> p q c", p=P)
                                 ).then_inc(b_ea[u], 16)

            steps(sp, step_ea)

            sp.wait_ge(need1_ready, 5)

            def load_agg(i, s):
                sp.wait_ge(agg_landed, sp.value_load(need[0:1, 1, bass.ds(i, 1)], min_val=1, max_val=STEPS))
                if isinstance(i, int) and i == STEPS - 1:
                    sp.dma_start(agg[s][0:PREST, :], node_rest(agg_d)).then_inc(b_agg[s], 16)
                else:
                    sp.dma_start(agg[s][:, :], node_chunk(agg_d, i)).then_inc(b_agg[s], 16)

            for i in range(2):
                load_x(x1_d, i, 0, i, b_x)

            def step_b(i, k, u):
                if real(i + 1):
                    wait(sp, bd.p1, i)
                    load_agg(i + 1, (u + 1) % 2)
                if real(i - 1):
                    sp.wait_ge(bd.out, i)
                if real(i + 3):
                    load_x(x1_d, i + 3, k + (u + 3) // UNROLL, (u + 3) % UNROLL, b_x)
                if real(i - 1):
                    store_x(res[(u + 1) % 2], out, i - 1, (u - 1) % UNROLL, b_stored)

            steps(sp, step_b, lead=1, lag=1)
            for u in range(UNROLL):
                sp.wait_ge(b_stored[u], 16 * ((STEPS - 1 - u) // UNROLL + 1))

        def norm_sum(dve, s, i, xv, st):
            wait(dve, s.xc, i)
            nc.vector.tensor_reduce(st[:, 0, :], xv, AX.X, ALU.add).then_inc(s.sum, 1)

        def norm_center(dve, s, i, xv, st, centered):
            n = xv.shape[1]
            wait(dve, s.h, i - 1)
            dve.wait_ge(s.sum, i + 1)
            nc.vector.scalar_tensor_tensor(out=centered[:, :].rearrange("p (g d) -> p g d", d=D),
                                           in0=st[:, 0, :].unsqueeze(2).to_broadcast([P, n, D]), scalar=-1.0 / D,
                                           in1=xv, op0=ALU.mult, op1=ALU.add).then_inc(s.xc, 1)

        def norm_square(act, s, i, centered, squared):
            act.wait_ge(s.xc, i + 1)
            wait(act, s.ss, i)
            nc.scalar.activation(squared[:, :], centered[:, :], ACT.Square, scale=D ** -0.5).then_inc(s.sq, 1)

        def norm_var(dve, s, i, squared, st):
            dve.wait_ge(s.sq, i + 1)
            nc.vector.tensor_reduce(st[:, 1, :], squared[:, :].rearrange("p (g d) -> p g d", d=D), AX.X,
                                    ALU.add).then_inc(s.ss, 1)

        def norm_std(act, s, i, st):
            act.wait_ge(s.ss, i + 1)
            nc.scalar.activation(st[:, 1, :], st[:, 1, :], ACT.Sqrt, bias=eps[:, 0:1]).then_inc(s.std, 1)

        def norm_rstd(dve, s, i, st):
            dve.wait_ge(s.std, i + 1)
            nc.vector.reciprocal(st[:, 2, :], st[:, 1, :]).then_inc(s.rstd, 1)

        def rows(t):
            return t[:, :].rearrange("p (g d) -> p g d", d=D)

        def norm_relu(dve, s, i, centered, st, to, done=None):
            n = st.shape[2]
            dve.wait_ge(s.rstd, i + 1)
            nc.vector.scalar_tensor_tensor(out=to, in0=rows(centered), scalar=0.0,
                                           in1=st[:, 2, :].unsqueeze(2).to_broadcast([P, n, D]),
                                           op0=ALU.max, op1=ALU.mult).then_inc(done or s.h, 1)

        def transposes(to, of, n, done):
            for j in range(n):
                last = nc.tensor.transpose(to[:, j * P:(j + 1) * P], of[:, j * P:(j + 1) * P], ident[:, :])
            last.then_inc(done, 1)

        def dst_columns(i, b):
            return nc.vector.tensor_copy(cols[b][:, :, :], dst_pair[:, bass.ds(i * Q, Q), :])

        def dst_rows(pe, s, i, b):
            pe.wait_ge(s.cols, i + 1)
            wait(pe, s.same, i)
            for q in range(Q):
                last = nc.tensor.transpose(psD[:, q * P:(q + 1) * P], cols[b][:, q, 0:1].to_broadcast([P, P]),
                                           ident[:, :])
            last.then_inc(s.dstb, 1)

        def dst_compare(dve, s, i, b, m):
            dve.wait_ge(s.dstb, i + 1)
            wait(dve, s.run_pe, Q * (i + 1 - UNROLL))
            nc.vector.tensor_tensor(
                same[m][:, :, :, :],
                psD[:, :].rearrange("p (q o e) -> p q o e", q=Q, o=1).to_broadcast([P, Q, 2, P]),
                cols[b][:, :, :].unsqueeze(3).to_broadcast([P, Q, 2, P]), ALU.is_equal).then_inc(s.same, 1)

        def dst_sums(pe, s, i, b, m, tiles):
            pe.wait_ge(s.same, i + 1)
            pe.wait_ge(s.msg, i + 1)
            for q in tiles:
                to = psR[:, q * R1:(q + 1) * R1]
                before = run[b][:, q - 1, :] if q else run[1 - b][:, Q - 1, :]
                wait(pe, s.run, i * Q + q)
                nc.tensor.matmul(to, same[m][:, q, 0, :], msg[b][:, q, :], start=True, stop=False)
                nc.tensor.matmul(to, same[m][:, q, 1, :], before, start=False, stop=True).then_inc(s.run_pe, 1)

        def dst_sums_out(act, s, i, b, tiles):
            wait(act, s.rows, i - 1)
            for q in tiles:
                act.wait_ge(s.run_pe, i * Q + q + 1)
                nc.scalar.copy(run[b][:, q, :], psR[:, q * R1:(q + 1) * R1]).then_inc(s.run, 1)

        def degree(dve, s, i, b, op, by):
            if real(i):
                dve.wait_ge(s.run, (i + 1) * Q)
                nc.vector.tensor_scalar(rdeg[:, 0:Q], run[b][:, :, D], by, None, op).then_inc(s.deg, 1)

        def degree_inverse(dve, s, i):
            if real(i):
                dve.wait_ge(s.deg, i + 1)
                nc.vector.reciprocal(rdeg[:, Q:2 * Q], rdeg[:, 0:Q]).then_inc(s.rdeg, 1)

        def dst_rows_out(dve, s, i, b):
            if real(i):
                dve.wait_ge(s.rdeg, i + 1)
                nc.vector.tensor_tensor(edge_rows[:, bass.ds(i * QD, QD)].rearrange("p (q d) -> p q d", d=D),
                                        run[b][:, :, 0:D], rdeg[:, Q:2 * Q].unsqueeze(2).to_broadcast([P, Q, D]),
                                        ALU.mult).then_inc(s.rows, 1)

        @block.gpsimd
        def _(pool):
            nc.gpsimd.memset(ident[:, :], 1.0).then_inc(pool_const, 1)
            nc.gpsimd.memset(sel[:, :], 1.0).then_inc(pool_const, 1)
            nc.gpsimd.iota(spare_i[:, :], [[P, T]], base=N, channel_multiplier=1).then_inc(pool_const, 1)
            nc.gpsimd.iota(bound_i[:, :], [[CHUNK, STEPS]], base=CHUNK, channel_multiplier=0).then_inc(pool_const, 1)
            pool.wait_ge(pool_const, 4)
            nc.gpsimd.affine_select(out=ident[:, :], in_=ident[:, :], pattern=[[-1, P]], compare_op=ALU.is_equal,
                                    fill=0.0, base=0, channel_multiplier=1).then_inc(pool_const, 1)
            nc.gpsimd.affine_select(out=sel[:, 0:1], in_=sel[:, 0:1], pattern=[[0, 1]], compare_op=ALU.is_equal,
                                    fill=0.0, base=1 - P, channel_multiplier=1).then_inc(pool_const, 1)

            def gather(table, j, landed):
                wait(pool, landed[j % UNROLL], 16 * Q * (j // UNROLL))
                for t in range(j * Q, (j + 1) * Q):
                    nc.gpsimd.indirect_dma_start(
                        out=edge_rows[:, t * D:(t + 1) * D], out_offset=None, in_=table,
                        in_offset=bass.IndirectOffsetOnAxis(ap=src_idx[:, t:t + 1], axis=0)
                    ).then_inc(landed[j % UNROLL], 16)

            def scatter(table, j, landed, op):
                wait(pool, landed[j % UNROLL], 16 * Q * (j // UNROLL))
                for t in range(j * Q, (j + 1) * Q):
                    nc.gpsimd.indirect_dma_start(
                        out=table, out_offset=bass.IndirectOffsetOnAxis(ap=end_idx[:, t:t + 1], axis=0),
                        in_=edge_rows[:, t * D:(t + 1) * D], in_offset=None, compute_op=op
                    ).then_inc(landed[j % UNROLL], 16)

            pool.wait_ge(idx_ready, 1)
            for j in range(STEPS):
                gather(x[:, :], j, a_gath)
            pool.wait_ge(idx_ready, 2)
            pool.wait_ge(need0_ready, 4)
            for j in range(STEPS):
                if j % UNROLL == 0:
                    last = min(j + UNROLL, STEPS) - 1
                    pool.wait_ge(x1_landed, pool.value_load(need[0:1, 0, last:last + 1], min_val=1, max_val=STEPS))
                    nc.gpsimd.nop(nofuse=True)
                pool.wait_ge(x1_landed, j + 1)
                pool.wait_ge(ae.rows, j + 1)
                scatter(x1_d[:, :], j, a_scat, ALU.add)
            for u in range(UNROLL):
                pool.wait_ge(a_scat[u], 16 * Q * ((STEPS - 1 - u) // UNROLL + 1))
            for j in range(STEPS):
                gather(x1_d[:, :], j, b_gath)
            pool.wait_ge(agg_zeroed, 16 * STEPS)
            for j in range(STEPS):
                pool.wait_ge(be.rows, j + 1)
                if j >= UNROLL:
                    pool.wait_ge(b_scat[j % UNROLL], 16 * Q * (j // UNROLL))
                    pool.sem_inc(agg_landed, 1)
                scatter(agg_d[:, :], j, b_scat, ALU.bypass)
            for j in range(STEPS - UNROLL, STEPS):
                pool.wait_ge(b_scat[j % UNROLL], 16 * Q * (j // UNROLL + 1))
                pool.sem_inc(agg_landed, 1)

        @block.vector
        def _(dve):
            for k, pad in enumerate((0, SENT, SENT)):
                nc.vector.memset(rows_i[k][:, :], pad).then_inc(filled, 1)
            nc.vector.memset(w_raw[:, :, :], 0.0).then_inc(filled, 1)
            for t, v in fills:
                nc.vector.memset(t[:], v).then_inc(filled, 1)
            nc.vector.memset(run[1][:, :, :], 0.0).then_inc(run_filled, 1)
            for k in range(2):
                nc.vector.memset(msg[k][:, :, D:R1], 1.0).then_inc(run_filled, 1)

            dve.wait_ge(rows_loaded[0], 16 * 3)
            nc.vector.tensor_copy(rows_f[0][:, :], rows_i[0][:, :]).then_inc(rows_conv, 1)
            dve.wait_ge(idxT, 1)
            nc.vector.tensor_copy(src_idx[:, :], psH[:, 0:T]).then_inc(idx_ready, 1)

            dve.wait_ge(bias_loaded, 32)
            for part in range(3):
                wait(dve, bias_split, 3 * part)
                nc.vector.tensor_copy(parts[:, :, part, :, :],
                                      (left if part else brow)[:, :, :].unsqueeze(2).to_broadcast([1, 2, NBLK, D])
                                      ).then_inc(bias_split, 1)
                if part < 2:
                    dve.wait_ge(bias_split, 3 * part + 1)
                    nc.vector.tensor_tensor(left[:, :, :], (left if part else brow)[:, :, :],
                                            parts[:, :, part, 0, :], ALU.subtract).then_inc(bias_split, 2)

            for k in range(1, 3):
                dve.wait_ge(rows_loaded[k], 16 * 3)
                nc.vector.tensor_copy(rows_f[k][:, :], rows_i[k][:, :]).then_inc(rows_conv, 1)
            dve.wait_ge(pool_const, 6)
            nc.vector.tensor_copy(spare_f[:, :], spare_i[:, :]).then_inc(prep, 1)
            nc.vector.tensor_scalar(sel[:, 1:2], sel[:, 0:1], 1.0, None, ALU.subtract).then_inc(prep, 1)
            dve.wait_ge(idxT, 2)
            nc.vector.tensor_copy(dst_f[:, :], psE[:, 0:T]).then_inc(prep, 1)
            nc.vector.tensor_copy(dst_pair[:, :, 0], psE[:, 0:T]).then_inc(prep, 1)
            dve.wait_ge(idxT, 3)
            nc.vector.tensor_copy(next_f[:, :], psR[:, 0:T]).then_inc(prep, 1)
            nc.vector.memset(dst_pair[:, 0:1, 1], -1.0).then_inc(prep, 1)
            dve.wait_ge(prep, 6)
            nc.vector.tensor_scalar(dst_pair[:, 1:T, 1], dst_f[:, 0:T - 1], sel[:, 0:1], sel[:, 1:2],
                                    ALU.mult, ALU.add).then_inc(prep, 1)
            dve.wait_ge(prep, 7)
            nc.vector.tensor_tensor(next_f[:, :], next_f[:, :], dst_f[:, :], ALU.not_equal).then_inc(prep, 1)
            nc.vector.tensor_tensor(dst_f[:, :], dst_f[:, :], spare_f[:, :], ALU.subtract).then_inc(prep, 1)
            dve.wait_ge(prep, 9)
            nc.vector.tensor_tensor(dst_f[:, :], dst_f[:, :], next_f[:, :], ALU.mult).then_inc(prep, 1)
            dve.wait_ge(prep, 10)
            nc.vector.tensor_tensor(end_idx[:, :], dst_f[:, :], spare_f[:, :], ALU.add).then_inc(idx_ready, 1)

            dve.wait_ge(w_pe, 1)
            nc.vector.tensor_copy(w_bd[:, :, :], psT[0][:, 0:2 * P].rearrange("p (a c) -> p a c", a=2)
                                  ).then_inc(w_prep, 1)

            def needs_of_x1():
                nc.vector.tensor_copy(first_i[:, 0:STEPS], dst_pair[0:1, 0:T:Q, 0]).then_inc(need0_ready, 1)
                nc.vector.memset(first_i[:, STEPS:STEPS + 1], SENT).then_inc(need0_ready, 1)
                dve.wait_ge(need0_ready, 2)
                nc.vector.tensor_scalar(chunk_i[:, :], first_i[:, 1:STEPS + 1], CHUNK.bit_length() - 1, None,
                                        ALU.arith_shift_right).then_inc(need0_ready, 1)
                dve.wait_ge(need0_ready, 3)
                nc.vector.tensor_scalar(need[:, 0, :], chunk_i[:, :], 1, STEPS, ALU.add, ALU.min
                                        ).then_inc(need0_ready, 1)

            def needs_of_agg():
                nc.vector.tensor_copy(first_f[:, :], dst_pair[0:1, 0:T:Q, 0]).then_inc(need1_ready, 1)
                nc.vector.tensor_copy(bound_f[:, :], bound_i[:, :]).then_inc(need1_ready, 1)
                dve.wait_ge(need1_ready, 2)
                nc.vector.tensor_tensor(less[:, :, :], first_f[:, :].unsqueeze(1).to_broadcast([1, STEPS, STEPS]),
                                        bound_f[:, :].unsqueeze(2).to_broadcast([1, STEPS, STEPS]),
                                        ALU.is_lt).then_inc(need1_ready, 1)
                dve.wait_ge(need1_ready, 3)
                nc.vector.tensor_reduce(need_f[:, :], less[:, :, :], AX.X, ALU.add).then_inc(need1_ready, 1)
                dve.wait_ge(need1_ready, 4)
                nc.vector.tensor_scalar(need[:, 1, :], need_f[:, :], 1.0, None, ALU.max).then_inc(need1_ready, 1)

            def weights_layer2():
                dve.wait_ge(wb_loaded, 16 * WB_DMAS)
                nc.vector.tensor_tensor(b2sum[:, :], b2c[:, 0:1].to_broadcast([D, P]),
                                        b2c[:, 1:2].to_broadcast([D, P]), ALU.add).then_inc(w_prep, 1)
                dve.wait_ge(w_pe, 2)
                nc.vector.tensor_copy(w2t[:, :], psT[1][0:D, 0:P]).then_inc(w_prep, 1)
                dve.wait_ge(w_pe, 3)
                nc.vector.tensor_copy(w2u[:, :], psY[:, 0:D]).then_inc(w_prep, 1)
                nc.vector.tensor_copy(b2u[:, 0, :], psY[0:1, D:2 * D]).then_inc(w_prep, 1)
                for part in range(3):
                    of = b2u[:, min(part, 1):min(part, 1) + 1, :]
                    dve.wait_ge(*((b2u_split, 2 * part) if part else (w_prep, 5)))
                    nc.vector.tensor_copy(b2u_parts[:, part, :, :], of.to_broadcast([1, Q, D])).then_inc(b2u_split, 1)
                    if part < 2:
                        dve.wait_ge(b2u_split, 2 * part + 1)
                        nc.vector.tensor_tensor(b2u[:, 1:2, :], of, b2u_parts[:, part, 0:1, :], ALU.subtract
                                                ).then_inc(b2u_split, 1)

            def edge_view(i):
                return edge_rows[:, bass.ds(i * QD, QD)].rearrange("p (q d) -> p q d", d=D)

            def node_view(u):
                return xin[u][:, :].rearrange("p (g d) -> p g d", d=D)

            def sums_a(i, k, u):
                if real(i):
                    dve.wait_ge(a_x[u], 16 * (k + 1))
                    norm_sum(dve, ad, i, node_view(u), stat)
                    dve.wait_ge(a_gath[u], 16 * Q * (k + 1))
                    norm_sum(dve, ae, i, edge_view(i), state)

            def center_a(i, u):
                if real(i):
                    norm_center(dve, ad, i, node_view(u), stat, xc[u % 2])
                    norm_center(dve, ae, i, edge_view(i), state, xce[u % 2])

            def columns(s, i, b):
                if real(i):
                    wait(dve, s.same, i - 1)
                    dst_columns(i, b).then_inc(s.cols, 1)

            def step_a(i, k, u):
                b = u % 2
                center_a(i + 1, (u + 1) % UNROLL)
                degree(dve, ae, i - 3, 1 - b, ALU.max, 1.0)
                if real(i - 1):
                    dst_compare(dve, ae, i - 1, 1 - b, (u - 1) % UNROLL)
                columns(ae, i, b)
                if real(i + 1):
                    norm_var(dve, ad, i + 1, sq, stat)
                    norm_var(dve, ae, i + 1, sqe, state)
                degree_inverse(dve, ae, i - 3)
                if real(i + 1):
                    norm_rstd(dve, ae, i + 1, stats)
                dst_rows_out(dve, ae, i - 3, 1 - b)
                if real(i + 1):
                    wait(dve, ad.tr1, i)
                    norm_relu(dve, ae, i + 1, xc[1 - b], stat, rows(h[1 - b]), ad.h)
                    wait(dve, ae.tr, i)
                    norm_relu(dve, ae, i + 1, xce[1 - b], state, rows(he[1 - b]))
                sums_a(i + 2, k + (u + 2) // UNROLL, (u + 2) % UNROLL)
                if isinstance(i, int) and i == 2:
                    needs_of_x1()

            steps(dve, step_a, lead=2, lag=3)
            weights_layer2()
            needs_of_agg()

            def sums_be(i, k, u):
                if real(i):
                    dve.wait_ge(b_gath[u], 16 * Q * (k + 1))
                    norm_sum(dve, be, i, edge_view(i), state)

            def center_be(i, b):
                if real(i):
                    norm_center(dve, be, i, edge_view(i), state, xce[b])

            def step_be(i, k, u):
                b = u % 2
                columns(be, i, b)
                if real(i + 1):
                    norm_var(dve, be, i + 1, sqe, state)
                center_be(i + 2, b)
                if real(i - 1):
                    dst_compare(dve, be, i - 1, 1 - b, (u - 1) % UNROLL)
                degree(dve, be, i - 3, 1 - b, ALU.add, 1e-8)
                if real(i + 1):
                    norm_rstd(dve, be, i + 1, state)
                degree_inverse(dve, be, i - 3)
                dst_rows_out(dve, be, i - 3, 1 - b)
                if real(i + 1):
                    wait(dve, be.tr, i + 2 - UNROLL)
                    norm_relu(dve, be, i + 1, xce[1 - b], state, comb[(u + 1) % UNROLL][:, :, 0:D])
                sums_be(i + 3, k + (u + 3) // UNROLL, (u + 3) % UNROLL)

            steps(dve, step_be, lead=3)

            def sums_bd(i, k, u):
                if real(i):
                    dve.wait_ge(b_x[u], 16 * (k + 1))
                    norm_sum(dve, bd, i, node_view(u), stat)

            def center_bd(i, u):
                if real(i):
                    norm_center(dve, bd, i, node_view(u), stat, xc[u % 2])

            def finish_bd(i, u, half):
                if real(i):
                    cols_of = slice(half * 512, (half + 1) * 512)
                    dve.wait_ge((bd.y0, bd.y1)[half], i + 1)
                    nc.vector.tensor_tensor(res[u % 2][:, cols_of], psY[:, cols_of], xin[u][:, cols_of], ALU.add
                                            ).then_inc((bd.out0, bd.out)[half], 1)

            def step_bd(i, k, u):
                center_bd(i + 1, (u + 1) % UNROLL)
                if real(i - 1):
                    wait(dve, b_stored[(u + 1) % UNROLL], 16 * (k + (u - 3) // UNROLL + 1))
                for half in range(2):
                    finish_bd(i - 1, (u - 1) % UNROLL, half)
                if real(i + 1):
                    norm_var(dve, bd, i + 1, sq, stat)
                sums_bd(i + 2, k + (u + 2) // UNROLL, (u + 2) % UNROLL)
                if real(i + 1):
                    norm_rstd(dve, bd, i + 1, stat)
                    wait(dve, bd.tr1, i)
                    norm_relu(dve, bd, i + 1, xc[(u + 1) % 2], stat, rows(h[(u + 1) % 2]))

            step(step_bd, -2)
            step(step_bd, -1)
            for i in range(STEPS, STEPS + 3):
                step(step_be, i)
            steps(dve, step_bd, lag=1)

        @block.scalar
        def _(act):
            def node_square(s, i, b):
                if real(i):
                    norm_square(act, s, i, xc[b], sq)

            def edge_square(s, i, b):
                if real(i):
                    norm_square(act, s, i, xce[b], sqe)

            def transposed_out(s, i, b, half):
                act.wait_ge((s.tr0, s.tr1)[half], i + 1)
                nc.scalar.copy(hT[b][:, half * 512:(half + 1) * 512], psT[half][:, :]
                               ).then_inc((s.hT0, s.hT1)[half], 1)

            def x1_out(i, u, half):
                act.wait_ge((ad.y0, ad.y1)[half], i + 1)
                nc.scalar.copy(res[u % 2][:, half * 512:(half + 1) * 512], psY[:, half * 512:(half + 1) * 512]
                               ).then_inc((ad.x1_0, ad.x1)[half], 1)

            def msg_a(i, b):
                act.wait_ge(ae.w, i + 1)
                wait(act, ae.run_pe, Q * (i - 1))
                if isinstance(i, int) and i < 2:
                    act.wait_ge(run_filled, RUN_FILLED)
                nc.scalar.copy(msg[b][:, :, 0:D], psH[:, 0:QD].rearrange("p (q d) -> p q d", d=D)
                               ).then_inc(ae.msg, 1)

            def step_a(i, k, u):
                b = u % 2
                if real(i):
                    wait(act, ad.y1, i - 1)
                    transposed_out(ad, i, b, 0)
                    transposed_out(ad, i, b, 1)
                    act.wait_ge(ae.tr, i + 1)
                    wait(act, ae.w, i - 1)
                    nc.scalar.copy(hTe[b][:, :], psE[:, 0:QD]).then_inc(ae.hT, 1)
                if real(i - 2):
                    dst_sums_out(act, ae, i - 2, b, range(0, 1))
                node_square(ad, i + 1, 1 - b)
                edge_square(ae, i + 1, 1 - b)
                if real(i - 2):
                    dst_sums_out(act, ae, i - 2, b, range(1, 2))
                if real(i - 1):
                    msg_a(i - 1, 1 - b)
                    wait(act, a_stored[(u + 1) % UNROLL], 16 * (k + (u - 3) // UNROLL + 1))
                    x1_out(i - 1, (u - 1) % UNROLL, 0)
                if real(i - 2):
                    dst_sums_out(act, ae, i - 2, b, range(2, 3))
                if real(i + 1):
                    act.wait_ge(ad.ss, i + 2)
                    norm_std(act, ae, i + 1, stats)
                if real(i - 1):
                    x1_out(i - 1, (u - 1) % UNROLL, 1)
                if real(i - 2):
                    dst_sums_out(act, ae, i - 2, b, range(3, 4))

            steps(act, step_a, lead=1, lag=2)

            def step_be(i, k, u):
                b = u % 2
                if real(i + 1):
                    norm_std(act, be, i + 1, state)
                if real(i):
                    act.wait_ge(be.tr, i + 1)
                    wait(act, be.hid_pe, i - 1)
                    nc.scalar.copy(hT[b][0:C, 0:Q * P], psT[b][0:C, :]).then_inc(be.hT, 1)
                if real(i - 2):
                    dst_sums_out(act, be, i - 2, b, range(0, 1))
                edge_square(be, i + 2, b)
                if real(i - 1):
                    act.wait_ge(be.hid_pe, i)
                    wait(act, be.w, i - 2)
                    nc.scalar.activation(hid[1 - b][:, :], psH[:, :], ACT.Relu, bias=b1c[:, 0:1]
                                         ).then_inc(be.hid, 1)
                if real(i - 2):
                    dst_sums_out(act, be, i - 2, b, range(1, 3))
                if real(i - 1):
                    act.wait_ge(be.w, i)
                    wait(act, be.run_pe, Q * (i - 2))
                    nc.scalar.copy(msg[1 - b][:, :, 0:D], psY[:, 0:QD].rearrange("p (q d) -> p q d", d=D)
                                   ).then_inc(be.msg, 1)
                if real(i - 2):
                    dst_sums_out(act, be, i - 2, b, range(3, 4))

            steps(act, step_be, lead=2)

            def step_bd(i, k, u):
                b = u % 2
                node_square(bd, i + 1, 1 - b)
                if real(i):
                    wait(act, bd.p1, i - 1)
                    for half in range(2):
                        transposed_out(bd, i, b, half)
                if real(i + 1):
                    norm_std(act, bd, i + 1, stat)
                for half in range(2):
                    if real(i):
                        act.wait_ge((bd.p0, bd.p1)[half], i + 1)
                        wait(act, (bd.y0, bd.y1)[half], i)
                        nc.scalar.activation(hid[half][:, :], psP[half][:, :], ACT.Relu, bias=ub1c[:, 0:1]
                                             ).then_inc((bd.r0, bd.r1)[half], 1)

            step(step_bd, -1)
            for i in range(STEPS, STEPS + 2):
                step(step_be, i)
            steps(act, step_bd)

        @block.tensor
        def _(pe):
            pe.wait_ge(pool_const, 6)
            for k, to in enumerate((psH, psE, psR)):
                pe.wait_ge(rows_conv, k + 1)
                for a in range(2):
                    last = nc.tensor.transpose(to[:, a * H:(a + 1) * H], rows_f[k][:, a * P:(a + 1) * P],
                                               ident[0:H, 0:H])
                last.then_inc(idxT, 1)
            pe.wait_ge(wa_loaded, 16 * WA_DMAS)
            for half in range(2):
                last = nc.tensor.transpose(psT[0][:, half * P:(half + 1) * P], w_raw[:, half, :], ident[:, :])
            last.then_inc(w_pe, 1)
            pe.wait_ge(w_prep, 1)
            pe.wait_ge(idx_ready, 2)

            def weights_layer2():
                pe.wait_ge(wb_loaded, 16 * WB_DMAS)
                nc.tensor.transpose(psT[1][0:D, 0:P], w2[:, :], ident[:, :]).then_inc(w_pe, 1)
                pe.wait_ge(w_prep, 3)
                nc.tensor.matmul(psY[:, 0:D], w2t[:, :], u1b[:, :], start=True, stop=True)
                nc.tensor.matmul(psY[:, D:2 * D], b2sum[:, :], u1b[:, :], start=True, stop=True).then_inc(w_pe, 1)
                pe.wait_ge(w_prep, 5)

            def norm_transposes(s, i, b):
                pe.wait_ge(s.h, i + 1)
                for half in range(2):
                    wait(pe, (s.hT0, s.hT1)[half], i)
                    transposes(psT[half], h[b][:, half * 512:(half + 1) * 512], 4, (s.tr0, s.tr1)[half])

            def by_nodes(s, i, half, source, weights, bias, ready, done, read, add=None):
                to = psY[:, half * 512:(half + 1) * 512]
                wait(pe, read, i)
                nc.tensor.matmul(to, ones3[:, :], bias3[:, bias, :], start=True, stop=False)
                if add is not None:
                    nc.tensor.matmul(to, ident[:, :], add[:, half * 512:(half + 1) * 512], start=False, stop=False)
                pe.wait_ge(ready, i + 1)
                for j in range(4):
                    last = nc.tensor.matmul(to[:, j * P:(j + 1) * P], source[:, j * P:(j + 1) * P], weights,
                                            start=False, stop=j == 3)
                last.then_inc(done, 1)

            pe.wait_ge(bias_moved, 16 * 6)

            def step_a(i, k, u):
                b = u % 2
                if real(i):
                    norm_transposes(ad, i, b)
                    pe.wait_ge(ae.h, i + 1)
                    wait(pe, ae.hT, i)
                    transposes(psE[:, 0:QD], he[b], 2, ae.tr)
                if real(i - 2):
                    dst_sums(pe, ae, i - 2, b, (u - 2) % UNROLL, range(0, 1))
                if real(i - 1):
                    pe.wait_ge(ae.hT, i)
                    wait(pe, ae.msg, i - 1)
                    for j in range(2):
                        last = nc.tensor.matmul(psH[:, j * P:(j + 1) * P], hTe[1 - b][:, j * P:(j + 1) * P],
                                                w_bd[:, 1, :], start=True, stop=True)
                    last.then_inc(ae.w, 1)
                if real(i - 2):
                    dst_sums(pe, ae, i - 2, b, (u - 2) % UNROLL, range(1, 2))
                for half in range(2):
                    if real(i - 1):
                        by_nodes(ad, i - 1, half, hT[1 - b][:, half * 512:(half + 1) * 512], w_bd[:, 0, :], 0,
                                 (ad.hT0, ad.hT1)[half], (ad.y0, ad.y1)[half], (ad.x1_0, ad.x1)[half],
                                 xin[(u - 1) % UNROLL])
                    if real(i - 2):
                        dst_sums(pe, ae, i - 2, b, (u - 2) % UNROLL, range(2 + half, 3 + half))
                    if real(i) and half == 0:
                        dst_rows(pe, ae, i, b)

            steps(pe, step_a, lag=2)
            weights_layer2()

            def step_be(i, k, u):
                b = u % 2
                if real(i):
                    pe.wait_ge(be.h, i + 1)
                    pe.wait_ge(b_ea[u], 16 * (k + (2 if isinstance(i, int) and i == STEPS - 1 else 1)))
                    wait(pe, be.hT, i - 1)
                    for q in range(Q):
                        last = nc.tensor.transpose(psT[b][0:C, q * P:(q + 1) * P], comb[u][:, q, :], ident[:, :])
                    last.then_inc(be.tr, 1)
                if real(i - 2):
                    dst_sums(pe, be, i - 2, b, (u - 2) % UNROLL, range(0, 1))
                if real(i - 1):
                    pe.wait_ge(be.hT, i)
                    wait(pe, be.hid, i - 1)
                    nc.tensor.matmul(psH[:, :], w1[:, :], hT[1 - b][0:C, 0:Q * P], start=True, stop=True
                                     ).then_inc(be.hid_pe, 1)
                if real(i):
                    dst_rows(pe, be, i, b)
                if real(i - 2):
                    dst_sums(pe, be, i - 2, b, (u - 2) % UNROLL, range(1, 2))
                if real(i - 1):
                    wait(pe, be.msg, i - 1)
                    nc.tensor.matmul(psY[:, 0:QD], ones3[:, :], b2u3[:, :], start=True, stop=False)
                    pe.wait_ge(be.hid, i)
                for q in range(Q):
                    if real(i - 1):
                        last = nc.tensor.matmul(psY[:, q * D:(q + 1) * D], hid[1 - b][:, q * P:(q + 1) * P], w2u[:, :],
                                                start=False, stop=q == Q - 1)
                        if q == Q - 1:
                            last.then_inc(be.w, 1)
                    if real(i - 2) and q % 2 == 1:
                        dst_sums(pe, be, i - 2, b, (u - 2) % UNROLL, range(2 + q // 2, 3 + q // 2))

            pe.wait_ge(b2u_moved, 16 * 3)
            steps(pe, step_be, lag=2)

            def step_bd(i, k, u):
                b = u % 2
                if real(i - 1):
                    for half in range(2):
                        by_nodes(bd, i - 1, half, hid[half], u2_bd[:, :], 1, (bd.r0, bd.r1)[half],
                                 (bd.y0, bd.y1)[half], (bd.out0, bd.out)[half])
                if real(i):
                    norm_transposes(bd, i, b)
                    pe.wait_ge(b_agg[b], 16 * (k * 2 + u // 2 + 1))
                    for half in range(2):
                        wait(pe, (bd.r0, bd.r1)[half], i)
                        for j in range(4):
                            at = half * 512 + j * P
                            nc.tensor.matmul(psP[half][:, j * P:(j + 1) * P], agg[b][:, at:at + P], ident[:, :],
                                             start=j == 0, stop=False)
                    for half in range(2):
                        pe.wait_ge((bd.hT0, bd.hT1)[half], i + 1)
                        nc.tensor.matmul(psP[half][:, :], u1_bd[:, :], hT[b][:, half * 512:(half + 1) * 512],
                                         start=False, stop=True).then_inc((bd.p0, bd.p1)[half], 1)

            steps(pe, step_bd, lag=1)


_INS = ['x', 'src', 'dst', 'edge_attr_32', 'L0_gnn_W', 'L0_gnn_b', 'L1_gnn_msg_w1', 'L1_gnn_msg_b1',
        'L1_gnn_msg_w2', 'L1_gnn_msg_b2', 'L1_gnn_upd_w1', 'L1_gnn_upd_b1', 'L1_gnn_upd_w2', 'L1_gnn_upd_b2']


def kernel(**inputs):
    import numpy as _np
    import concourse.bacc as _bacc
    from concourse import mybir as _mybir
    from concourse.bass_utils import run_bass_kernel_spmd as _run

    nc = _bacc.Bacc("TRN2", target_bir_lowering=False, num_devices=1)
    arrays, args = {}, []
    for name in _INS:
        a = _np.ascontiguousarray(inputs[name])
        arrays[f"in_{name}"] = a
        args.append(nc.dram_tensor(f"in_{name}", a.shape, _mybir.dt.from_np(a.dtype), kind="ExternalInput").ap())
    shape = inputs['x'].shape
    args.append(nc.dram_tensor("out", shape, _mybir.dt.float32, kind="ExternalOutput").ap())
    gnn_program(nc, *args)
    r = _run(nc, [arrays], core_ids=[0])
    return r.results[0]["out"]
```
